# Optimizing a Trainium2 kernel written in Bass

```python
import numpy as np
import jax
import jax.numpy as jnp

def _softmax(x, axis=-1):
    return jax.nn.softmax(x, axis=axis)

def _gelu(x):
    return jax.nn.gelu(x, approximate=True)

def _silu(x):
    return jax.nn.silu(x)

def _sigmoid(x):
    return jax.nn.sigmoid(x)

def _layernorm(x, axis=-1, eps=1e-05):
    m = jnp.mean(x, axis=axis, keepdims=True)
    v = jnp.var(x, axis=axis, keepdims=True)
    return (x - m) / jnp.sqrt(v + eps)

def _scatter_add(tgt, idx, src, axis=0):
    return tgt.at[idx].add(src)

def _segment_sum(src, seg, n):
    return jax.ops.segment_sum(src, seg, n)
kernel_name = 'mk_xattn_ffn_d1_seqx_r8_f7d4ae'

def setup_inputs(seed: int=0):
    np.random.seed(seed)
    _w = jnp.asarray

    def _rec_inputs():
        import jax
        import jax.numpy as jnp
        _rk = jax.random.key(seed)
        x = -0.0002928 + 1 * jax.random.normal(jax.random.fold_in(_rk, 1), (64, 128, 128), jnp.float32)
        _lenS = 128 - jax.random.randint(jax.random.fold_in(_rk, 7), (64,), 0, max(1, 128 // 4) + 1, jnp.int32)
        _lenS2 = 120 - jax.random.randint(jax.random.fold_in(_rk, 8), (64,), 0, max(1, 120 // 4) + 1, jnp.int32)
        _ctx_1024P = jax.random.normal(jax.random.fold_in(_rk, 11), (64, 16, 128), jnp.float32)
        _ctx_1024c = jax.random.dirichlet(jax.random.fold_in(_rk, 511), 0.3 * jnp.ones((16,), jnp.float32), (64, 120))
        _ctx_1024t = jnp.einsum('bsk,bkd->bsd', _ctx_1024c, _ctx_1024P)
        _ctx_1024t = _ctx_1024t * jax.lax.rsqrt(jnp.mean(jnp.square(_ctx_1024t)) + 1e-12) * 0.953939
        ctx_1024 = -1.39393e-06 + 0.999914 * (_ctx_1024t + 0.3 * jax.random.normal(jax.random.fold_in(_rk, 611), (64, 120, 128), jnp.float32))
        fside_1x1xSxS2_0 = 0.000675642 + 1.00031 * jax.random.normal(jax.random.fold_in(_rk, 12), (1, 1, 128, 120), jnp.float32)
        return (x, ctx_1024, fside_1x1xSxS2_0)
    x, ctx_1024, fside_1x1xSxS2_0 = _rec_inputs()

    def _L0_xattn_setup():
        import jax, jax.numpy as jnp
        import numpy as np
        D_MODEL = 128
        N_HEAD = 16
        D_KEY = 64
        D_VALUE = 64

        def _split_heads(x, n_head, d_head):
            B, S, _ = x.shape
            return x.reshape(B, S, n_head, d_head).transpose(0, 2, 1, 3)
        key = jax.random.key(seed)
        ks = jax.random.split(key, 8)
        B, S = (2, 256)
        queries = jax.random.normal(ks[0], (B, S, D_MODEL), dtype=jnp.float32)
        keys = jax.random.normal(ks[1], (B, S, D_MODEL), dtype=jnp.float32)
        values = jax.random.normal(ks[2], (B, S, D_MODEL), dtype=jnp.float32)
        attn_bias = jax.random.normal(ks[3], (1, 1, S, S), dtype=jnp.float32)
        s = 1.0 / np.sqrt(D_MODEL)
        Wq = jax.random.normal(ks[4], (N_HEAD * D_KEY, D_MODEL), dtype=jnp.float32) * s
        Wk = jax.random.normal(ks[5], (N_HEAD * D_KEY, D_MODEL), dtype=jnp.float32) * s
        Wv = jax.random.normal(ks[6], (N_HEAD * D_VALUE, D_MODEL), dtype=jnp.float32) * s
        Wp = jax.random.normal(ks[7], (D_MODEL, N_HEAD * D_VALUE), dtype=jnp.float32) * s
        return {'queries': queries, 'keys': keys, 'values': values, 'attn_bias': attn_bias, 'Wq': Wq, 'Wk': Wk, 'Wv': Wv, 'Wp': Wp}
    _L0_xattn_all = _L0_xattn_setup()
    _L0_xattn_in = {k: v for k, v in _L0_xattn_all.items() if k in ('Wq', 'Wk', 'Wv', 'Wp')}
    del _L0_xattn_all

    def _L0_ffn_setup():
        import jax, jax.numpy as jnp
        import numpy as np
        CAPACITY = 2
        B, S, D, E, I = (4, 512, 128, 8, 512)
        key = jax.random.key(seed)
        k0, k1, k2, k3, k4 = jax.random.split(key, 5)
        x = jax.random.normal(k0, (B, S, D), dtype=jnp.float32)
        gate_w = jax.random.normal(k1, (E, D), dtype=jnp.float32) * 0.006
        w_gate = jax.random.normal(k2, (E, I, D), dtype=jnp.float32) * (1.0 / np.sqrt(D))
        w_up = jax.random.normal(k3, (E, I, D), dtype=jnp.float32) * (1.0 / np.sqrt(D))
        w_down = jax.random.normal(k4, (E, D, I), dtype=jnp.float32) * (1.0 / np.sqrt(I))
        return {'x': x, 'gate_w': gate_w, 'w_gate': w_gate, 'w_up': w_up, 'w_down': w_down}
    _L0_ffn_all = _L0_ffn_setup()
    _L0_ffn_in = {k: v for k, v in _L0_ffn_all.items() if k in ('gate_w', 'w_gate', 'w_up', 'w_down')}
    del _L0_ffn_all
    return {'x': x, 'ctx_1024': ctx_1024, 'fside_1x1xSxS2_0': fside_1x1xSxS2_0, 'L0_xattn_Wq': _L0_xattn_in['Wq'], 'L0_xattn_Wk': _L0_xattn_in['Wk'], 'L0_xattn_Wv': _L0_xattn_in['Wv'], 'L0_xattn_Wp': _L0_xattn_in['Wp'], 'L0_ffn_gate_w': _L0_ffn_in['gate_w'], 'L0_ffn_w_gate': _L0_ffn_in['w_gate'], 'L0_ffn_w_up': _L0_ffn_in['w_up'], 'L0_ffn_w_down': _L0_ffn_in['w_down']}

def reference(x, ctx_1024, fside_1x1xSxS2_0, L0_xattn_Wq, L0_xattn_Wk, L0_xattn_Wv, L0_xattn_Wp, L0_ffn_gate_w, L0_ffn_w_gate, L0_ffn_w_up, L0_ffn_w_down):
    import jax
    import jax.numpy as jnp

    def _L0_xattn_ref(queries, keys, values, attn_bias, Wq, Wk, Wv, Wp):
        import jax, jax.numpy as jnp
        import numpy as np
        D_MODEL = 128
        N_HEAD = 16
        D_KEY = 64
        D_VALUE = 64

        def _split_heads(x, n_head, d_head):
            B, S, _ = x.shape
            return x.reshape(B, S, n_head, d_head).transpose(0, 2, 1, 3)
        q = _split_heads(queries @ Wq.T, N_HEAD, D_KEY)
        k = _split_heads(keys @ Wk.T, N_HEAD, D_KEY)
        v = _split_heads(values @ Wv.T, N_HEAD, D_VALUE)
        scores = jnp.einsum('bhqd,bhkd->bhqk', q, k) * D_MODEL ** (-0.5) + attn_bias
        weights = jax.nn.softmax(scores, axis=-1)
        out = jnp.einsum('bhqk,bhkd->bhqd', weights, v)
        B, H, Sq, Dv = out.shape
        out = out.transpose(0, 2, 1, 3).reshape(B, Sq, H * Dv)
        return out @ Wp.T

    def _L0_ffn_ref(x, gate_w, w_gate, w_up, w_down):
        import jax, jax.numpy as jnp
        import numpy as np
        CAPACITY = 2
        B, S, D = x.shape
        E = gate_w.shape[0]
        k = S // E * CAPACITY
        logits = jnp.einsum('bsd,ed->bse', x, gate_w)
        affinity = jax.nn.softmax(logits, axis=-1)
        affinity = jnp.transpose(affinity, (0, 2, 1))
        gating, idx = jax.lax.top_k(affinity, k)
        bidx = jnp.arange(B)[:, None, None]
        x_in = x[bidx, idx]
        h = jax.nn.silu(jnp.einsum('bekd,eid->beki', x_in, w_gate)) * jnp.einsum('bekd,eid->beki', x_in, w_up)
        x_e = jnp.einsum('beki,edi->bekd', h, w_down)
        out = jnp.zeros_like(x).at[bidx, idx].add(gating[..., None] * x_e)
        return out
    x = x + _L0_xattn_ref(_layernorm(x, axis=-1), ctx_1024, ctx_1024, fside_1x1xSxS2_0, L0_xattn_Wq, L0_xattn_Wk, L0_xattn_Wv, L0_xattn_Wp)
    x = x + _L0_ffn_ref(_layernorm(x, axis=-1), L0_ffn_gate_w, L0_ffn_w_gate, L0_ffn_w_up, L0_ffn_w_down)
    return x

_drawn_inputs = setup_inputs


def setup_inputs(seed=0):
    import zlib

    import numpy as np

    out = dict(_drawn_inputs(seed))
    spreads = {}
    factors = {}
    for name, (base, spread) in spreads.items():
        noise = np.random.default_rng([zlib.crc32(name.encode()), seed]).standard_normal(out[name].shape)
        drawn = base * np.exp(spread * noise) if base else spread * noise
        out[name] = jnp.asarray(drawn.astype(out[name].dtype))
    for name, factor in factors.items():
        out[name] = (out[name] * factor).astype(out[name].dtype)
    return out
```

```python
from contextlib import ExitStack

import concourse.bass as bass
from concourse import mybir

ALU = mybir.AluOpType
ACT = mybir.ActivationFunctionType
AX = mybir.AxisListType.X
F32 = mybir.dt.float32
F16 = mybir.dt.float16
U32 = mybir.dt.uint32

EPS = 1e-5
WSCALE = 16.0
FRONT = 5
DRAIN = 3


def cross_attention_moe_kernel(nc, x, ctx_t, bias, wqkv_t, wp_t, gate_t, ffn_w, out):
    S, B, D = x.shape
    K = ctx_t.shape[2]
    HD = wqkv_t.shape[1] // 3
    PAIRS = wp_t.shape[1]
    H = 2 * PAIRS
    DH = HD // H
    GROUPS = 4
    GH = H // GROUPS
    GP = PAIRS // GROUPS
    E = gate_t.shape[1]
    I = ffn_w.shape[1] // (3 * E)
    CAP = S // E * 2
    WCH = ffn_w.shape[1] // B
    SCORE = float(D) ** -0.5 / (WSCALE * WSCALE)
    assert S == 128 and D == 128 and DH == 64 and B % 16 == 0 and CAP == 32

    QK = GP * (S + K)
    OW = DH + 1

    with ExitStack() as ctx:
        def sb(name, shape, dt):
            return ctx.enter_context(nc.sbuf_tensor(name, shape, dt))

        def sem(name):
            return ctx.enter_context(nc.semaphore(name))

        x_sb = sb("x_sb", [S, B, D], F32)
        xg_hi = sb("xg_hi", [S, B, D], F16)
        xg_lo = sb("xg_lo", [S, B, D], F16)
        ffn_hi = sb("ffn_hi", [D, 3 * E * I], F16)
        ffn_lo = sb("ffn_lo", [D, 3 * E * I], F16)
        logits = sb("logits", [S, B, E], F32)
        ident = sb("ident", [128, 128], F32)
        iota = sb("iota", [128, 128], F32)
        gate_sb = sb("gate_sb", [D, E], F32)

        pick = sb("pick", [128, B // 4, E], F32)
        gain = sb("gain", [128, B // 4, E], F32)

        attention(nc, locals())
        routing(nc, locals())
        experts(nc, locals())


def attention(nc, v):
    x, ctx_t, bias, wqkv_t, wp_t, gate_t, ffn_w = (v[n] for n in (
        "x", "ctx_t", "bias", "wqkv_t", "wp_t", "gate_t", "ffn_w"))
    S, B, D, K, HD, H, DH, E = (v[n] for n in ("S", "B", "D", "K", "HD", "H", "DH", "E"))
    PAIRS, GROUPS, GH, GP, WCH, SCORE, QK, OW = (v[n] for n in (
        "PAIRS", "GROUPS", "GH", "GP", "WCH", "SCORE", "QK", "OW"))
    x_sb, xg_hi, xg_lo, ffn_hi, ffn_lo, logits, ident, iota, gate_sb = (v[n] for n in (
        "x_sb", "xg_hi", "xg_lo", "ffn_hi", "ffn_lo", "logits", "ident", "iota", "gate_sb"))

    with ExitStack() as ctx:
        def sb(name, shape, dt):
            return ctx.enter_context(nc.sbuf_tensor(name, shape, dt))

        def two(name, shape, dt):
            return [sb(f"{name}{i}", shape, dt) for i in range(2)]

        def bank(name):
            return ctx.enter_context(nc.psum_tensor(name, [128, 512], F32))

        sem = v["sem"]

        w_hi = sb("w_hi", [D, 3 * HD], F16)
        w_lo = sb("w_lo", [D, 3 * HD], F16)
        wp_sb = sb("wp_sb", [2 * DH, PAIRS, D], F32)
        bias_sb = sb("bias_sb", [S, K], F32)
        half = sb("half", [128, 2], F32)
        ctx_f = two("ctx_f", [D, K], F32)
        ctx_hi = two("ctx_hi", [D, K], F16)
        ctx_lo = two("ctx_lo", [D, K], F16)
        wst = two("wst", [D, WCH], F32)
        wsc = sb("wsc", [D, WCH], F32)
        stats = sb("stats", [S, 2, 6], F32)
        mv = sb("mv", [S, 2, 2], F32)
        vpe = sb("vpe", [S, 2], F32)
        rstd = sb("rstd", [S, 2], F32)
        xn = sb("xn", [S, D], F32)
        xn2 = sb("xn2", [S, D], F32)
        xT_hi = two("xT_hi", [D, S], F16)
        xT_lo = two("xT_lo", [D, S], F16)
        x2T = sb("x2T", [D, S], F32)
        qk_hi = two("qk_hi", [128, GROUPS, QK], F16)
        qk_lo = two("qk_lo", [128, GROUPS, QK], F16)
        v_hi = two("v_hi", [128, H, OW], F16)
        v_lo = two("v_lo", [128, H, DH], F16)
        neg = two("neg", [S, GH, K], F32)
        negmax = two("negmax", [S, GH], F32)
        probs = two("probs", [S, GH, K], F32)
        pT_hi = two("pT_hi", [128, GH, S], F16)
        pT_lo = two("pT_lo", [128, GH, S], F16)
        rsum = sb("rsum", [S, GH], F32)
        o_sb = two("o_sb", [S, GH, DH], F32)
        oT = two("oT", [2 * DH, GP, S], F32)
        w_f = sb("w_f", [D, 3 * HD], F32)

        bk_s = [bank("bk_s0"), bank("bk_s1")]
        bk_t, bk_a, bk_b, bk_o, bk_x, bk_y = (bank(n) for n in (
            "bk_t", "bk_a", "bk_b", "bk_o", "bk_x", "bk_y"))

        loaded_w, loaded_b, loaded = sem("loaded_w"), sem("loaded_b"), sem("loaded")
        const_ready = sem("const_ready")
        w_hi_ready, w_ready = sem("w_hi_ready"), sem("w_ready")
        bias_ready = sem("bias_ready")
        ctx_ready, ffnw_ready = sem("ctx_ready"), sem("ffnw_ready")
        pool_chain, dve_chain = sem("pool_chain"), sem("dve_chain")
        stats_ready, rstd_ready = sem("stats_ready"), sem("rstd_ready")
        xn_ready, xn2_ready = sem("xn_ready"), sem("xn2_ready")
        xg_ready = sem("xg_ready")
        xT_written, x2T_written = sem("xT_written"), sem("x2T_written")
        xT_hi_ready, xT_lo_ready, x2T_ready = sem("xT_hi_ready"), sem("xT_lo_ready"), sem("x2T_ready")
        qk_written, qk_hi_ready, qk_lo_ready = sem("qk_written"), sem("qk_hi_ready"), sem("qk_lo_ready")
        v_written, v_hi_ready, v_lo_ready = sem("v_written"), sem("v_hi_ready"), sem("v_lo_ready")
        scores_written, neg_ready, probs_ready = sem("scores_written"), sem("neg_ready"), sem("probs_ready")
        pT_written, pT_hi_ready, pT_lo_ready = sem("pT_written"), sem("pT_hi_ready"), sem("pT_lo_ready")
        pv_written, o_ready = sem("pv_written"), sem("o_ready")
        oT_written, oT_ready = sem("oT_written"), sem("oT_ready")
        proj_written, x1_ready = sem("proj_written"), sem("x1_ready")
        logits_written, logits_ready = sem("logits_written"), sem("logits_ready")

        first, last = -1, B + DRAIN
        loop_end = B - 1
        assert (loop_end - FRONT) % 2 == 0

        def live(b):
            return not isinstance(b, int) or 0 <= b < B

        def upto(count):
            return min(count, B) if isinstance(count, int) else count

        def some(count):
            return not isinstance(count, int) or count > 0

        def alone(eng):
            eng.nop(nofuse=True)

        def slots(eng, slot, end=last, loop_end=loop_end, first=first):
            for t in range(first, FRONT):
                slot(t, t % 2)
            with eng.Fori(FRONT, loop_end - 1, 2) as t:
                slot(t, FRONT % 2)
                slot(t + 1, (FRONT + 1) % 2)
            for t in range(loop_end, end):
                slot(t, t % 2)

        def behind(t, g, k):
            return t - 1 + (g - k) // GROUPS, (g - k) % GROUPS

        block = ctx.enter_context(nc.Block())

        @block.sync
        def _(sp):
            def slot(t, par):
                if some(t * 48):
                    sp.wait_ge(loaded, t * 48)
                sp.dma_start(x_sb[:, t, :], x[:, t, :]).then_inc(loaded, 16)
                if some(t - 1):
                    sp.wait_ge(ctx_ready, t - 1)
                sp.dma_start(ctx_f[par][:, :], ctx_t[:, t, :]).then_inc(loaded, 16)
                if some(t - 1):
                    sp.wait_ge(ffnw_ready, t - 1)
                src = ffn_w[:, bass.ds(t * WCH, WCH)] if not isinstance(t, int) else ffn_w[:, t * WCH:(t + 1) * WCH]
                sp.dma_start(wst[par][:, :], src).then_inc(loaded, 16)

            slots(sp, slot, end=B, first=0)

        @block.gpsimd
        def _(pool):
            pool.memset(ident[:, :], 0.0).then_inc(pool_chain, 1)
            pool.memset(half[:, :], -0.5).then_inc(const_ready, 1)
            pool.memset(vpe[:, :], 1.0).then_inc(const_ready, 1)
            pool.memset(mv[:, :, :], 1.0).then_inc(const_ready, 1)
            for i in range(2):
                pool.memset(v_hi[i][:, :, DH:OW], 1.0).then_inc(const_ready, 1)
            pool.wait_ge(pool_chain, 1)
            pool.affine_select(out=ident[:, :], in_=ident[:, :], compare_op=ALU.not_equal, fill=1.0,
                               base=0, pattern=[[-1, 128]], channel_multiplier=1).then_inc(const_ready, 1)
            pool.iota(iota[:, :], pattern=[[1, 128]], base=0, channel_multiplier=0,
                      allow_small_or_imprecise_dtypes=True).then_inc(const_ready, 1)
            pool.wait_ge(const_ready, 7)

            def split(src, hi, lo, done):
                pool.tensor_copy(hi, src).then_inc(pool_chain, 1)
                return lambda: pool.tensor_tensor(lo, src, hi, ALU.subtract).then_inc(done, 1)

            def slot(t, par):
                c = chain(t)
                pool.wait_ge(stats_ready, t + 2)
                alone(pool)
                pool.tensor_scalar(vpe[:, :], mv[:, :, 1], EPS, None, ALU.add).then_inc(pool_chain, 1)
                pool.wait_ge(pool_chain, c[0])
                if some(upto(t + 1)):
                    pool.wait_ge(xn_ready, upto(t + 1))
                if some(t - 3):
                    pool.wait_ge(xn2_ready, t - 3)
                pool.tensor_tensor(rstd[:, :], vpe[:, :], half[:, :], ALU.pow).then_inc(rstd_ready, 1)
                if live(t + 1):
                    pool.wait_ge(loaded, (t + 2) * 48)
                    if some(4 * t):
                        pool.wait_ge(v_written, 4 * t)
                    i = (par + 1) % 2
                    alone(pool)
                    pool.tensor_copy(ctx_hi[i][:, :], ctx_f[i][:, :]).then_inc(pool_chain, 1)
                    pool.wait_ge(pool_chain, c[1])
                    pool.tensor_tensor(ctx_lo[i][:, :], ctx_f[i][:, :], ctx_hi[i][:, :],
                                       ALU.subtract).then_inc(ctx_ready, 1)
                if live(t):
                    if some(t):
                        pool.wait_ge(ffnw_ready, t)
                    alone(pool)
                    pool.tensor_scalar(wsc[:, :], wst[par][:, :], WSCALE, None, ALU.mult).then_inc(pool_chain, 1)
                    pool.wait_ge(pool_chain, c[2])
                    at = bass.ds(t * WCH, WCH) if not isinstance(t, int) else slice(t * WCH, (t + 1) * WCH)
                    alone(pool)
                    pool.tensor_copy(ffn_hi[:, at], wsc[:, :]).then_inc(pool_chain, 1)
                    pool.wait_ge(pool_chain, c[3])
                    pool.tensor_tensor(ffn_lo[:, at], wsc[:, :], ffn_hi[:, at], ALU.subtract).then_inc(ffnw_ready, 1)
                if live(t - 3):
                    pool.wait_ge(xn2_ready, t - 2)
                    alone(pool)
                    pool.tensor_copy(xg_hi[:, t - 3, :], xn2[:, :]).then_inc(pool_chain, 1)
                    pool.wait_ge(pool_chain, c[4])
                    pool.tensor_tensor(xg_lo[:, t - 3, :], xn2[:, :], xg_hi[:, t - 3, :],
                                       ALU.subtract).then_inc(xg_ready, 1)

            def chain(t):
                def before(t, lag, each):
                    return each * (t - lag) if not isinstance(t, int) else each * min(max(t - lag, 0), B)
                c = 1 + before(t, -1, 1) if not isinstance(t, int) else 1 + (t + 1)
                c = c + before(t, -1, 1) + before(t, 0, 2) + before(t, 3, 1)
                out = [c + 1]
                for part, k in ((t + 1, 1), (t, 2), (t - 3, 1)):
                    for _ in range(k):
                        out.append(out[-1] + (1 if live(part) else 0))
                return out

            slots(pool, slot)

        @block.scalar
        def _(act):
            act.dma_start(w_f[:, :], wqkv_t).then_inc(loaded_w, 16)
            act.dma_start(bias_sb[:, :], bias).then_inc(loaded_b, 16)
            act.dma_start(wp_sb[:, :, :], wp_t).then_inc(loaded_b, 16)
            act.dma_start(gate_sb[:, :], gate_t).then_inc(loaded_b, 16)
            act.wait_ge(loaded_w, 16)
            nc.scalar.activation(w_hi[:, :], w_f[:, :], ACT.Copy, scale=WSCALE).then_inc(w_hi_ready, 1)

            def step(t, par, g):
                n = 4 * (t - 1) + g
                b1, g1 = behind(t, g, 1)
                if live(b1):
                    act.wait_ge(pT_written, 4 * b1 + g1 + 1)
                    if some(4 * b1 + g1 - 1):
                        act.wait_ge(pv_written, 4 * b1 + g1 - 1)
                    nc.scalar.copy(pT_hi[g1 % 2][0:K, :, :].rearrange("p a b -> p (a b)"),
                                   bk_t[0:K, :]).then_inc(pT_hi_ready, 1)
                if live(t - 1):
                    act.wait_ge(neg_ready, n + 1)
                    if some(n - 1):
                        act.wait_ge(pT_written, n - 1)
                    for i in range(GH):
                        e = nc.scalar.activation(probs[g % 2][:, i, :], neg[g % 2][:, i, :], ACT.Exp,
                                                 bias=negmax[g % 2][:, i:i + 1], scale=-1.0)
                    e.then_inc(probs_ready, 1)
                if live(t):
                    act.wait_ge(qk_written, 4 * t + g + 1)
                    if some(4 * (t - 2) + g + 1):
                        act.wait_ge(scores_written, 4 * (t - 2) + g + 1)
                    nc.scalar.copy(qk_hi[par][:, g, :], bk_a[:, 0:QK]).then_inc(qk_hi_ready, 1)
                if g == GROUPS - 1 and live(t - 3):
                    act.wait_ge(logits_written, t - 2)
                    if live(t):
                        act.wait_ge(v_written, 4 * t + g + 1)
                    nc.scalar.copy(logits[:, t - 3, :], bk_b[:, 256:256 + E]).then_inc(logits_ready, 1)
                if live(t):
                    act.wait_ge(v_written, 4 * t + g + 1)
                    if some(4 * (t - 2) + g + 1):
                        act.wait_ge(pv_written, 4 * (t - 2) + g + 1)
                    nc.scalar.copy(v_hi[par][0:K, GH * g:GH * (g + 1), 0:DH],
                                   bk_b[0:K, 0:GH * DH].rearrange("p (a b) -> p a b", a=GH)).then_inc(v_hi_ready, 1)
                b3, g3 = behind(t, g, 3)
                if g == 2:
                    if live(t + 1):
                        act.wait_ge(xT_written, t + 2)
                    if live(t - 3):
                        act.wait_ge(x2T_written, t - 2)
                if live(b3):
                    act.wait_ge(oT_written, 4 * b3 + g3 + 1)
                    if some(4 * b3 + g3 - 1):
                        act.wait_ge(proj_written, 4 * b3 + g3 - 1)
                    nc.scalar.copy(oT[g3 % 2][:, :, :].rearrange("p a b -> p (a b)"),
                                   bk_x[:, 0:GP * S]).then_inc(oT_ready, 1)
                if g == 2 and live(t - 3):
                    if some(t - 3):
                        act.wait_ge(logits_written, t - 3)
                    nc.scalar.copy(x2T[:, :], bk_x[:, 384:512]).then_inc(x2T_ready, 1)
                if g == 2 and live(t + 1):
                    if some(4 * t):
                        act.wait_ge(qk_written, 4 * t)
                    nc.scalar.copy(xT_hi[(par + 1) % 2][:, :], bk_x[:, 256:384]).then_inc(xT_hi_ready, 1)

            slots(act, lambda t, par: [step(t, par, g) for g in range(GROUPS)])

        @block.vector
        def _(dve):
            dve.wait_ge(loaded_b, 48)
            nc.vector.tensor_scalar(bias_sb[:, :], bias_sb[:, :], 1.0 / SCORE, None,
                                    ALU.mult).then_inc(bias_ready, 1)
            dve.wait_ge(w_hi_ready, 1)
            nc.vector.scalar_tensor_tensor(out=w_lo[:, :], in0=w_f[:, :], scalar=WSCALE, in1=w_hi[:, :],
                                           op0=ALU.mult, op1=ALU.subtract).then_inc(w_ready, 1)
            dve.wait_ge(bias_ready, 1)
            dve.wait_ge(const_ready, 7)

            def chain(t):
                if not isinstance(t, int):
                    return (t + 1) + (t - 3) + 4 * (t - 1) - 2
                part = lambda lag: min(max(t - lag, 0), B)
                return part(-1) + part(3) + max(min(4 * (t - 1) - 2, 4 * B), 0)

            def step(t, par, g, c):
                n = 4 * (t - 1) + g
                if live(t - 1):
                    dve.wait_ge(scores_written, n + 1)
                    if some(n - 1):
                        dve.wait_ge(probs_ready, n - 1)
                    alone(dve)
                    for i in range(GH):
                        r = nc.vector.tensor_tensor_reduce(
                            out=neg[g % 2][:, i, :], in0=bk_s[i % 2][:, (i // 2) * K:(i // 2 + 1) * K],
                            in1=bias_sb[:, :], scale=-SCORE, scalar=3.0e38, op0=ALU.add, op1=ALU.min,
                            accum_out=negmax[g % 2][:, i:i + 1])
                    r.then_inc(neg_ready, 1)
                if g == 0 and live(t - 3):
                    dve.wait_ge(proj_written, 4 * (t - 3) + 4)
                    nc.vector.tensor_tensor(x_sb[:, t - 3, :], x_sb[:, t - 3, :], bk_y[:, 0:D],
                                            ALU.add).then_inc(x1_ready, 1)
                    dve.wait_ge(x1_ready, t - 2)
                    alone(dve)
                    nc.vector.bn_stats(stats[:, 1, :], x_sb[:, t - 3, :]).then_inc(dve_chain, 1)
                    c = c + 1
                if g == 0 and live(t + 1):
                    dve.wait_ge(loaded, (t + 2) * 48)
                    alone(dve)
                    nc.vector.bn_stats(stats[:, 0, :], x_sb[:, t + 1, :]).then_inc(dve_chain, 1)
                    c = c + 1
                if g == 0:
                    if some(c):
                        dve.wait_ge(dve_chain, c)
                    if some(t + 1):
                        dve.wait_ge(rstd_ready, t + 1)
                    parts = [k for k, b in ((0, t + 1), (1, t - 3)) if live(b)]
                    alone(dve)
                    for k in parts:
                        a = nc.vector.bn_aggr(mv[:, k, :], stats[:, k, :])
                    a.then_inc(stats_ready, 1)
                b1, g1 = behind(t, g, 1)
                if live(b1):
                    dve.wait_ge(pT_hi_ready, 4 * b1 + g1 + 1)
                    if some(4 * b1 + g1 - 1):
                        dve.wait_ge(pv_written, 4 * b1 + g1 - 1)
                    nc.vector.tensor_tensor(pT_lo[g1 % 2][0:K, :, :].rearrange("p a b -> p (a b)"), bk_t[0:K, :],
                                            pT_hi[g1 % 2][0:K, :, :].rearrange("p a b -> p (a b)"),
                                            ALU.subtract).then_inc(pT_lo_ready, 1)
                b2, g2 = behind(t, g, 2)
                if live(b2):
                    dve.wait_ge(pv_written, 4 * b2 + g2 + 1)
                    o = bk_o[:, 0:GH * OW].rearrange("p (a b) -> p a b", a=GH)
                    nc.vector.reciprocal(rsum[:, :], o[:, :, DH]).then_inc(dve_chain, 1)
                    c = c + 1
                    if some(c):
                        dve.wait_ge(dve_chain, c)
                    if some(4 * b2 + g2 - 1):
                        dve.wait_ge(oT_written, 4 * b2 + g2 - 1)
                    nc.vector.scalar_tensor_tensor(
                        out=o_sb[g2 % 2][:, :, :], in0=o[:, :, 0:DH], scalar=1.0 / WSCALE,
                        in1=rsum[:, :].rearrange("p (a b) -> p a b", b=1).to_broadcast([S, GH, DH]),
                        op0=ALU.mult, op1=ALU.mult).then_inc(o_ready, 1)
                if live(t):
                    dve.wait_ge(qk_hi_ready, 4 * t + g + 1)
                    if some(4 * (t - 2) + g + 1):
                        dve.wait_ge(scores_written, 4 * (t - 2) + g + 1)
                    nc.vector.tensor_tensor(qk_lo[par][:, g, :], bk_a[:, 0:QK], qk_hi[par][:, g, :],
                                            ALU.subtract).then_inc(qk_lo_ready, 1)
                    dve.wait_ge(v_hi_ready, 4 * t + g + 1)
                    if some(4 * (t - 2) + g + 1):
                        dve.wait_ge(pv_written, 4 * (t - 2) + g + 1)
                    nc.vector.tensor_tensor(v_lo[par][0:K, GH * g:GH * (g + 1), :],
                                            bk_b[0:K, 0:GH * DH].rearrange("p (a b) -> p a b", a=GH),
                                            v_hi[par][0:K, GH * g:GH * (g + 1), 0:DH],
                                            ALU.subtract).then_inc(v_lo_ready, 1)
                if g == 1:
                    dve.wait_ge(rstd_ready, t + 2)
                    if live(t + 1):
                        dve.wait_ge(xT_written, t + 1)
                        nc.vector.tensor_scalar(xn[:, :], x_sb[:, t + 1, :], mv[:, 0, 0:1], rstd[:, 0:1],
                                                ALU.subtract, ALU.mult).then_inc(xn_ready, 1)
                    if live(t - 3):
                        if some(t - 3):
                            dve.wait_ge(x2T_written, t - 3)
                        if some(t - 3):
                            dve.wait_ge(xg_ready, t - 3)
                        nc.vector.tensor_scalar(xn2[:, :], x_sb[:, t - 3, :], mv[:, 1, 0:1], rstd[:, 1:2],
                                                ALU.subtract, ALU.mult).then_inc(xn2_ready, 1)
                if g == 2 and live(t + 1):
                    dve.wait_ge(xT_hi_ready, t + 2)
                    if some(4 * t):
                        dve.wait_ge(qk_written, 4 * t)
                    i = (par + 1) % 2
                    nc.vector.tensor_tensor(xT_lo[i][:, :], bk_x[:, 256:384], xT_hi[i][:, :],
                                            ALU.subtract).then_inc(xT_lo_ready, 1)
                return c

            def slot(t, par):
                c = chain(t)
                for g in range(GROUPS):
                    c = step(t, par, g, c)

            slots(dve, slot)

        @block.tensor
        def _(pe):
            pe.wait_ge(const_ready, 7)
            pe.wait_ge(loaded_b, 48)

            def product(out, lhs, rhs, **kw):
                (lh, ll), (rh, rl) = lhs, rhs
                nc.tensor.matmul(out, lh, rh, start=True, stop=False)
                nc.tensor.matmul(out, ll, rh, start=False, stop=False)
                return nc.tensor.matmul(out, lh, rl, start=False, stop=True)

            def step(t, par, g):
                n = 4 * (t - 1) + g
                if live(t - 1):
                    p1 = (par + 1) % 2
                    pe.wait_ge(qk_lo_ready, n + 1)
                    if some(n):
                        pe.wait_ge(neg_ready, n)
                    for j in range(GP):
                        for lo_q, lo_k in ((0, 0), (1, 0), (0, 1)):
                            for h in range(2):
                                r = slice(DH * h, DH * (h + 1))
                                q = (qk_hi, qk_lo)[lo_q][p1][r, g, j * S:(j + 1) * S]
                                k = (qk_hi, qk_lo)[lo_k][p1][r, g, GP * S + j * K:GP * S + (j + 1) * K]
                                m = nc.tensor.matmul(bk_s[h][:, j * K:(j + 1) * K], q, k,
                                                     start=lo_q + lo_k == 0, stop=lo_k == 1)
                    m.then_inc(scores_written, 1)
                b1, g1 = behind(t, g, 1)
                if live(b1):
                    pe.wait_ge(probs_ready, 4 * b1 + g1 + 1)
                    if some(4 * b1 + g1):
                        pe.wait_ge(pT_lo_ready, 4 * b1 + g1)
                    for i in range(GH):
                        m = nc.tensor.transpose(bk_t[0:K, i * S:(i + 1) * S], probs[g1 % 2][:, i, :], ident[:, :])
                    m.then_inc(pT_written, 1)
                b2, g2 = behind(t, g, 2)
                if live(b2):
                    p2 = (par + 1) % 2 if g >= 2 else par
                    pe.wait_ge(pT_lo_ready, 4 * b2 + g2 + 1)
                    pe.wait_ge(v_lo_ready, 4 * b2 + g2 + 1)
                    if some(4 * b2 + g2):
                        pe.wait_ge(o_ready, 4 * b2 + g2)
                    for i in range(GH):
                        h = GH * g2 + i
                        ph, pl = pT_hi[g2 % 2][0:K, i, :], pT_lo[g2 % 2][0:K, i, :]
                        nc.tensor.matmul(bk_o[:, i * OW:(i + 1) * OW], ph, v_hi[p2][0:K, h, :], start=True, stop=False)
                        nc.tensor.matmul(bk_o[:, i * OW:i * OW + DH], ph, v_lo[p2][0:K, h, :], start=False, stop=False)
                        m = nc.tensor.matmul(bk_o[:, i * OW:(i + 1) * OW], pl, v_hi[p2][0:K, h, :], start=False, stop=True)
                    m.then_inc(pv_written, 1)
                if live(t):
                    if g == 0:
                        if some(1):
                            pe.wait_ge(w_ready, 1)
                        pe.wait_ge(xT_lo_ready, t + 1)
                        pe.wait_ge(ctx_ready, t + 1)
                    if some(4 * t + g):
                        pe.wait_ge(qk_lo_ready, 4 * t + g)
                    xT = xT_hi[par][:, :], xT_lo[par][:, :]
                    cT = ctx_hi[par][:, :], ctx_lo[par][:, :]
                    for j in range(GP):
                        for base, at, wide, r in ((0, j * S, S, xT), (HD, GP * S + j * K, K, cT)):
                            c = base + 2 * DH * (GP * g + j)
                            w = w_hi[:, c:c + 2 * DH], w_lo[:, c:c + 2 * DH]
                            m = product(bk_a[:, at:at + wide], w, r)
                    m.then_inc(qk_written, 1)
                if g == 0:
                    if some(upto(t - 3)):
                        pe.wait_ge(logits_ready, upto(t - 3))
                if live(t):
                    if some(4 * t + g):
                        pe.wait_ge(v_lo_ready, 4 * t + g)
                if g == GROUPS - 1 and live(t - 3):
                    pe.wait_ge(x2T_ready, t - 2)
                    nc.tensor.matmul(bk_b[:, 256:256 + E], x2T[:, :], gate_sb[:, :],
                                     start=True, stop=True).then_inc(logits_written, 1)
                if live(t):
                    c = 2 * HD + GH * DH * g
                    product(bk_b[0:K, 0:GH * DH], cT, (w_hi[:, c:c + GH * DH], w_lo[:, c:c + GH * DH])
                            ).then_inc(v_written, 1)
                b3, g3 = behind(t, g, 3)
                if live(b3) or g == 2:
                    if live(b3) and some(4 * b3 + g3):
                        pe.wait_ge(oT_ready, 4 * b3 + g3)
                    if g == 3:
                        if live(t + 1) and some(t + 2):
                            pe.wait_ge(xT_lo_ready, t + 2)
                        if live(t - 3) and some(t - 2):
                            pe.wait_ge(x2T_ready, t - 2)
                    if g == 2:
                        if live(t) and some(t + 1):
                            pe.wait_ge(xT_lo_ready, t + 1)
                        if live(t - 3) and some(t - 3):
                            pe.wait_ge(x2T_ready, t - 3)
                        if live(t + 1):
                            pe.wait_ge(xn_ready, t + 2)
                            nc.tensor.transpose(bk_x[:, 256:384], xn[:, :], ident[:, :]).then_inc(xT_written, 1)
                        if live(t - 3):
                            pe.wait_ge(xn2_ready, t - 2)
                            nc.tensor.transpose(bk_x[:, 384:512], xn2[:, :], ident[:, :]).then_inc(x2T_written, 1)
                if live(b3):
                    pe.wait_ge(o_ready, 4 * b3 + g3 + 1)
                    for j in range(GP):
                        m = nc.tensor.transpose(bk_x[:, j * S:(j + 1) * S],
                                                o_sb[g3 % 2][:, 2 * j:2 * j + 2, :].rearrange("p a b -> p (a b)"),
                                                ident[:, :])
                    m.then_inc(oT_written, 1)
                b4, g4 = behind(t, g, 4)
                if live(b4):
                    pe.wait_ge(oT_ready, 4 * b4 + g4 + 1)
                    if g4 == 0:
                        if some(b4):
                            pe.wait_ge(x1_ready, b4)
                    for j in range(GP):
                        m = nc.tensor.matmul(bk_y[:, 0:D], oT[g4 % 2][:, j, :], wp_sb[:, GP * g4 + j, :],
                                             start=(g4 == 0 and j == 0), stop=(g4 == GROUPS - 1 and j == GP - 1))
                    m.then_inc(proj_written, 1)

            slots(pe, lambda t, par: [step(t, par, g) for g in range(GROUPS)])


def routing(nc, v):
    S, B, E, CAP, WSCALE_ = v["S"], v["B"], v["E"], v["CAP"], WSCALE
    logits, ident, pick, gain, sem = (v[n] for n in ("logits", "ident", "pick", "gain", "sem"))
    R = B // 16

    with ExitStack() as ctx:
        def sb(name, shape, dt):
            return ctx.enter_context(nc.sbuf_tensor(name, shape, dt))

        top = sb("top", [S, B], F32)
        shifted = sb("shifted", [S, B, E], F32)
        weights = sb("weights", [S, B, E], F32)
        total = sb("total", [S, B], F32)
        share = sb("share", [S, B], F32)
        aff = sb("aff", [S, R, 4, 4, E], F32)
        affT = sb("affT", [128, R, S], F32)
        vals = sb("vals", [128, R, CAP], F32)
        idx = sb("idx", [128, R, CAP], U32)
        idx_f = sb("idx_f", [128, R, CAP], F32)
        vals_T = sb("vals_T", [128, R, CAP], F32)
        bk_aff = ctx.enter_context(nc.psum_tensor("bk_aff", [128, R, S], F32))
        exp_ready, aff_ready, aff_written, chain = (sem(n) for n in (
            "exp_ready", "aff_ready", "aff_written", "routing_chain"))
        shifted_ready = sem("shifted_ready")

        block = ctx.enter_context(nc.Block())

        @block.scalar
        def _(act):
            act.wait_ge(shifted_ready, 1)
            nc.scalar.activation(weights[:, :, :], shifted[:, :, :], ACT.Exp).then_inc(exp_ready, 1)

        @block.tensor
        def _(pe):
            pe.wait_ge(aff_ready, 1)
            for r in range(R):
                m = nc.tensor.transpose(bk_aff[:, r, :], aff[:, r, :, :, :].rearrange("p a b c -> p (a b c)"),
                                        ident[:, :])
            m.then_inc(aff_written, 1)

        @block.vector
        def _(dve):
            count = [0]

            def done(instruction):
                count[0] += 1
                instruction.then_inc(chain, 1)
                dve.wait_ge(chain, count[0])

            def over_experts(a):
                return a.rearrange("p (a b) -> p a b", b=1).to_broadcast([S, B, E])

            done(nc.vector.tensor_reduce(top[:, :], logits[:, :, :], AX, ALU.max))
            nc.vector.tensor_tensor(shifted[:, :, :], logits[:, :, :], over_experts(top[:, :]),
                                    ALU.subtract).then_inc(shifted_ready, 1)
            dve.wait_ge(exp_ready, 1)
            done(nc.vector.tensor_reduce(total[:, :], weights[:, :, :], AX, ALU.add))
            done(nc.vector.reciprocal(share[:, :], total[:, :]))
            for r in range(R):
                at = slice(16 * r, 16 * (r + 1))
                a = nc.vector.tensor_tensor(
                    aff[:, r, :, :, :].rearrange("p q j e -> p j q e"),
                    weights[:, at, :].rearrange("p (j q) e -> p j q e", j=4),
                    share[:, at].rearrange("p (j q c) -> p j q c", j=4, c=1).to_broadcast([S, 4, 4, E]), ALU.mult)
            a.then_inc(aff_ready, 1)
            dve.wait_ge(aff_written, 1)
            done(nc.vector.tensor_copy(affT[:, :, :], bk_aff[:, :, :]))
            for k in range(CAP // 8):
                at = slice(8 * k, 8 * (k + 1))
                for r in range(R):
                    m = nc.vector.max(vals[:, r, at], affT[:, r, :])
                done(m)
                for r in range(R):
                    m = nc.vector.max_index(idx[:, r, at], vals[:, r, at], affT[:, r, :])
                done(m)
                for r in range(R):
                    m = nc.vector.match_replace(out=affT[:, r, :], in_to_replace=vals[:, r, at],
                                                in_values=affT[:, r, :], imm_value=-1.0)
                done(m)
            done(nc.vector.tensor_copy(idx_f[:, :, :], idx[:, :, :]))
            flat = lambda a: a.rearrange("p a b -> p (a b)")
            nc.vector.transpose(flat(pick[:, :, :]), flat(idx_f[:, :, :]))
            done(nc.vector.transpose(flat(vals_T[:, :, :]), flat(vals[:, :, :])))
            done(nc.vector.tensor_scalar(flat(gain[:, :, :]), flat(vals_T[:, :, :]), 1.0 / WSCALE, None, ALU.mult))


def experts(nc, v):
    S, B, D, E, I, CAP = (v[n] for n in ("S", "B", "D", "E", "I", "CAP"))
    x_sb, xg_hi, xg_lo, ffn_hi, ffn_lo, ident, iota, pick, gain, out, sem = (v[n] for n in (
        "x_sb", "xg_hi", "xg_lo", "ffn_hi", "ffn_lo", "ident", "iota", "pick", "gain", "out", "sem"))
    R = B // 16
    M = 4
    T = M * 4 * CAP
    IC = I // 128
    UP, DOWN = E * I, 2 * E * I

    with ExitStack() as ctx:
        def sb(name, shape, dt):
            return ctx.enter_context(nc.sbuf_tensor(name, shape, dt))

        def two(name, shape, dt):
            return [sb(f"{name}{i}", shape, dt) for i in range(2)]

        def bank(name, dt=F32):
            return ctx.enter_context(nc.psum_tensor(name, [128, 2048 // mybir.dt.size(dt)], dt))

        ident_h = sb("ident_h", [128, 128], F16)
        x_in = sb("x_in", [D, 2, 2, E, T], F16)
        hid = [[sb(f"hid{i}{j}", [128, IC, T], F16) for j in range(2)] for i in range(2)]
        silu = two("silu", [128, T], F32)
        hid_f = two("hid_f", [128, T], F32)
        y_f = sb("y_f", [128, T], F32)
        y = two("y", [128, E, M, D], F16)
        hot_t = sb("hot_t", [128, E, S], F16)
        hot = sb("hot", [S, E, 128], F16)
        back = sb("back", [128, M, E, S], F16)
        bk_g, bk_u = [bank("bk_g0"), bank("bk_g1")], [bank("bk_u0"), bank("bk_u1")]
        bk_y, bk_c, bk_x = bank("bk_y2"), bank("bk_c"), bank("bk_x2")
        bk_h = bank("bk_h")
        bk_q = (bk_c, bk_y, bk_h, bk_x)
        ident_ready = sem("ident_ready")
        gate_written, up_written, down_written = sem("gate_written"), sem("up_written"), sem("down_written")
        silu_ready, hid_f_ready = sem("silu_ready"), sem("hid_f_ready")
        hid_hi_ready, hid_lo_ready = sem("hid_hi_ready"), sem("hid_lo_ready")
        y_f_ready, y_hi_ready, y_lo_ready = sem("y_f_ready"), sem("y_hi_ready"), sem("y_lo_ready")
        hot_t_ready, hot_written, hot_ready = sem("hot_t_ready"), sem("hot_written"), sem("hot_ready")
        gather_written, x_in_ready = sem("gather_written"), sem("x_in_ready")
        back_ready, scatter_written, out_ready = sem("back_ready"), sem("scatter_written"), sem("out_ready")
        stored = sem("stored")

        def some(count):
            return not isinstance(count, int) or count > 0

        def each_quad(eng, quad):
            quad(0)
            with eng.Fori(1, M, 1) as m:
                quad(m)

        def rounds(eng, step, combine):
            def one(r, gather, scatter):
                for e in range(2):
                    step(r, e, e, gather)
                    if scatter and e == 0:
                        combine(r - 1)
                with eng.Fori(2, E - 1, 2) as e:
                    step(r, e, 0, gather)
                    step(r, e + 1, 1, gather)

            one(0, R > 1, False)
            if R > 2:
                with eng.Fori(1, R - 1, 1) as r:
                    one(r, True, True)
            if R > 1:
                one(R - 1, False, True)

        def quad_of(e, odd):
            if isinstance(e, int):
                return e // 2
            return (e - odd) // 2

        block = ctx.enter_context(nc.Block())

        @block.sync
        def _(sp):
            for r in range(R):
                sp.wait_ge(out_ready, M * (r + 1))
                sp.dma_start(out[:, 16 * r:16 * (r + 1), :], x_sb[:, 16 * r:16 * (r + 1), :]).then_inc(stored, 16)
            sp.wait_ge(stored, 16 * R)

        @block.tensor
        def _(pe):
            pe.wait_ge(ident_ready, 1)
            bk_h16 = bk_h[:, :].bitcast(F16)

            def scattered(r1, e):
                if not (isinstance(e, int) and e == 0):
                    if some(M * (r1 - 1)):
                        pe.wait_ge(out_ready, M * (r1 - 1))

            def turn(r1, m, e):
                a = 4 * r1 + m
                pe.wait_ge(hot_t_ready, a + 1)
                if some(a):
                    pe.wait_ge(hot_ready, a)
                scattered(r1, e)
                for e in range(E):
                    t = nc.tensor.transpose(bk_h16[:, e * 128:(e + 1) * 128], hot_t[:, e, :], ident_h[:, :])
                t.then_inc(hot_written, 1)

            def gather(r1, m, q, e):
                a = 4 * (4 * r1 + m) + q
                pe.wait_ge(hot_ready, 4 * r1 + m + 1)
                if some(a):
                    pe.wait_ge(x_in_ready, a)
                scattered(r1, e)
                rhs = hot[:, :, q * CAP:(q + 1) * CAP]
                b = 16 * r1 + 4 * m + q
                nc.tensor.matmul(bk_x[:, 0:E * CAP], xg_hi[:, b, :], rhs, start=True, stop=True)
                nc.tensor.matmul(bk_x[:, E * CAP:2 * E * CAP], xg_lo[:, b, :], rhs,
                                 start=True, stop=True).then_inc(gather_written, 1)

            def quad(m):
                turn(0, m, 0)
                for q in range(4):
                    gather(0, m, q, 0)

            def projections(r, e, n, ic):
                k = IC * n + ic
                if ic == 0:
                    pe.wait_ge(x_in_ready, 16 * (r + 1))
                par = r % 2
                for bk, written, free, base in ((bk_g, gate_written, silu_ready, 0), (bk_u, up_written, hid_f_ready, UP)):
                    if some(k - 1):
                        pe.wait_ge(free, k - 1)
                    at = bass.ds(base + e * I + ic * 128, 128)
                    o = bk[ic % 2][:, :]
                    hi, lo = x_in[:, par, 0, e, :], x_in[:, par, 1, e, :]
                    nc.tensor.matmul(o, ffn_hi[:, at], hi, start=True, stop=False)
                    nc.tensor.matmul(o, ffn_lo[:, at], hi, start=False, stop=False)
                    nc.tensor.matmul(o, ffn_hi[:, at], lo, start=False, stop=True).then_inc(written, 1)

            def down(n, e, par):
                pe.wait_ge(hid_lo_ready, IC * (n + 1))
                if some(n):
                    pe.wait_ge(y_f_ready, n)
                for m in range(M):
                    for ic in range(IC):
                        at = bass.ds(DOWN + e * I + ic * D, D)
                        o = bk_y[:, m * D:(m + 1) * D]
                        hh, hl = (hid[i][par][:, ic, m * 128:(m + 1) * 128] for i in range(2))
                        nc.tensor.matmul(o, hh, ffn_hi[:, at], start=ic == 0, stop=False)
                        nc.tensor.matmul(o, hl, ffn_hi[:, at], start=False, stop=False)
                        t = nc.tensor.matmul(o, hh, ffn_lo[:, at], start=False, stop=ic == IC - 1)
                t.then_inc(down_written, 1)

            def step(r, e, odd, with_gather):
                n = E * r + e
                m = quad_of(e, odd)
                projections(r, e, n, 0)
                if with_gather and odd:
                    gather(r + 1, m, 1, e)
                projections(r, e, n, 1)
                if with_gather:
                    gather(r + 1, m, 2, e) if odd else turn(r + 1, m, e)
                if not (isinstance(n, int) and n == 0):
                    before = e - 1 if not isinstance(e, int) or e > 0 else E - 1
                    if isinstance(e, int) and e == 1 or not isinstance(e, int):
                        if some(M * r):
                            pe.wait_ge(out_ready, M * r)
                    down(n - 1, before, 1 - odd)
                if with_gather:
                    gather(r + 1, m, 3 if odd else 0, e)
                projections(r, e, n, 2)
                projections(r, e, n, 3)

            def combine(r):
                pe.wait_ge(y_lo_ready, E * (r + 1))
                pe.wait_ge(y_f_ready, E * (r + 1))
                if not isinstance(r, int) or r < R - 1:
                    if not isinstance(r, int) or r + 2 < R:
                        pe.wait_ge(x_in_ready, 16 * (r + 2) + 1)
                        pe.wait_ge(hot_ready, 4 * (r + 2) + 1)
                    else:
                        pe.wait_ge(x_in_ready, 16 * R)
                        pe.wait_ge(hot_ready, 4 * R)
                pe.wait_ge(back_ready, M * (r + 1))
                for m in range(M):
                    for e in range(E):
                        for i in range(2):
                            for q in range(4):
                                rows = slice(32 * q, 32 * (q + 1))
                                t = nc.tensor.matmul(bk_q[q][:, m * D:(m + 1) * D], back[rows, m, e, :],
                                                     y[i][rows, e, m, :], start=e + i == 0,
                                                     stop=(e == E - 1 and i == 1))
                t.then_inc(scatter_written, 1)

            each_quad(pe, quad)
            rounds(pe, step, combine)
            down(E * R - 1, E - 1, 1)
            combine(R - 1)

        @block.scalar
        def _(act):
            def x_in_part(r1, m, q):
                a = 4 * (4 * r1 + m) + q
                act.wait_ge(gather_written, a + 1)
                if some(IC * E * (r1 - 1)):
                    act.wait_ge(up_written, IC * E * (r1 - 1))
                for i in range(2):
                    c = nc.scalar.copy(x_in[:, r1 % 2, i, :, bass.ds(m * 128 + q * CAP, CAP)],
                                       bk_x[:, i * E * CAP:(i + 1) * E * CAP].rearrange("p (a b) -> p a b", a=E))
                c.then_inc(x_in_ready, 1)

            def quad(m):
                for q in range(4):
                    x_in_part(0, m, q)

            def gate(n, ic):
                k = IC * n + ic
                act.wait_ge(gate_written, k + 1)
                if some(k - 1):
                    act.wait_ge(hid_f_ready, k - 1)
                nc.scalar.activation(silu[ic % 2][:, :], bk_g[ic % 2][:, :], ACT.Silu,
                                     scale=1.0 / WSCALE).then_inc(silu_ready, 1)

            def hid_hi(n, ic, par):
                k = IC * n + ic
                act.wait_ge(hid_f_ready, k + 1)
                nc.scalar.copy(hid[0][par][:, ic, :], hid_f[ic % 2][:, :]).then_inc(hid_hi_ready, 1)

            def y_hi(n, e):
                act.wait_ge(y_f_ready, n + 1)
                nc.scalar.copy(y[0][:, e, :, :].rearrange("p a b -> p (a b)"), y_f[:, :]).then_inc(y_hi_ready, 1)

            def step(r, e, odd, with_gather):
                n = E * r + e
                m = quad_of(e, odd)
                first = isinstance(n, int) and n == 0
                gate(n, 0)
                if not first:
                    hid_hi(n - 1, IC - 1, 1 - odd)
                if with_gather and odd:
                    x_in_part(r + 1, m, 1)
                gate(n, 1)
                hid_hi(n, 0, odd)
                if with_gather:
                    for q in (2, 3) if odd else (0,):
                        x_in_part(r + 1, m, q)
                gate(n, 2)
                hid_hi(n, 1, odd)
                if not first:
                    if isinstance(e, int) and e == 1 or not isinstance(e, int):
                        if some(r):
                            act.wait_ge(scatter_written, r)
                    y_hi(n - 1, e - 1 if not isinstance(e, int) or e > 0 else E - 1)
                gate(n, 3)
                hid_hi(n, 2, odd)

            each_quad(act, quad)
            rounds(act, step, lambda r: None)
            hid_hi(E * R - 1, IC - 1, 1)
            y_hi(E * R - 1, E - 1)

        @block.gpsimd
        def _(pool):
            pool.tensor_copy(ident_h[:, :], ident[:, :]).then_inc(ident_ready, 1)

            def hid_lo(n, ic, par):
                k = IC * n + ic
                pool.wait_ge(hid_hi_ready, k + 1)
                nc.gpsimd.tensor_tensor(hid[1][par][:, ic, :], hid_f[ic % 2][:, :], hid[0][par][:, ic, :],
                                        ALU.subtract).then_inc(hid_lo_ready, 1)

            def y_lo(n, e):
                pool.wait_ge(y_hi_ready, n + 1)
                part = [y[i][:, e, :, :].rearrange("p a b -> p (a b)") for i in range(2)]
                nc.gpsimd.tensor_tensor(part[1], y_f[:, :], part[0], ALU.subtract).then_inc(y_lo_ready, 1)

            def step(r, e, odd, with_gather):
                n = E * r + e
                first = isinstance(n, int) and n == 0
                if not first:
                    hid_lo(n - 1, IC - 1, 1 - odd)
                for ic in range(2):
                    hid_lo(n, ic, odd)
                if not first:
                    y_lo(n - 1, e - 1 if not isinstance(e, int) or e > 0 else E - 1)
                hid_lo(n, 2, odd)

            rounds(pool, step, lambda r: None)
            hid_lo(E * R - 1, IC - 1, 1)
            y_lo(E * R - 1, E - 1)

        @block.vector
        def _(dve):
            iota_e = iota[:, :].rearrange("p (a b) -> p a b", a=1).to_broadcast([128, E, S])

            def one_hot(dst, quad):
                return nc.vector.tensor_tensor(
                    dst, iota_e,
                    pick[:, quad, :].rearrange("p (a b) -> p a b", b=1).to_broadcast([128, E, S]), ALU.is_equal)

            def hot_rows(r1, m):
                a = 4 * r1 + m
                if some(a):
                    dve.wait_ge(hot_written, a)
                one_hot(hot_t[:, :, :], a).then_inc(hot_t_ready, 1)

            def hot_columns(r1, m):
                a = 4 * r1 + m
                dve.wait_ge(hot_written, a + 1)
                if some(4 * a):
                    dve.wait_ge(gather_written, 4 * a)
                nc.vector.tensor_copy(hot[:, :, :].rearrange("p a b -> p (a b)"),
                                      bk_h[:, :].bitcast(F16)).then_inc(hot_ready, 1)

            def quad(m):
                hot_rows(0, m)
                hot_columns(0, m)

            def hidden(n, ic):
                k = IC * n + ic
                dve.wait_ge(silu_ready, k + 1)
                dve.wait_ge(up_written, k + 1)
                if some(k - 1):
                    dve.wait_ge(hid_lo_ready, k - 1)
                nc.vector.tensor_tensor(hid_f[ic % 2][:, :], bk_u[ic % 2][:, :], silu[ic % 2][:, :],
                                        ALU.mult).then_inc(hid_f_ready, 1)

            def gated(n, r, e):
                dve.wait_ge(down_written, n + 1)
                if some(n):
                    dve.wait_ge(y_lo_ready, n)
                nc.vector.tensor_tensor(
                    y_f[:, :].rearrange("p (a b) -> p a b", a=M), bk_y[:, :].rearrange("p (a b) -> p a b", a=M),
                    gain[:, bass.ds(M * r, M), e].rearrange("p (a b) -> p a b", b=1).to_broadcast([128, M, D]),
                    ALU.mult).then_inc(y_f_ready, 1)

            def step(r, e, odd, with_gather):
                n = E * r + e
                m = quad_of(e, odd)
                if with_gather and not odd:
                    hot_rows(r + 1, m)
                hidden(n, 0)
                hidden(n, 1)
                if with_gather and not odd:
                    hot_columns(r + 1, m)
                if not (isinstance(n, int) and n == 0):
                    if isinstance(e, int) and e == 0:
                        gated(n - 1, r - 1, E - 1)
                    else:
                        gated(n - 1, r, e - 1)
                hidden(n, 2)
                if odd:
                    if some(r):
                        dve.wait_ge(scatter_written, r)
                    one_hot(back[:, m, :, :], M * r + m).then_inc(back_ready, 1)
                hidden(n, 3)

            def combine(r):
                dve.wait_ge(scatter_written, r + 1)
                for q in range(4):
                    at = x_sb[:, bass.ds(16 * r, 16), :].rearrange("p (a b) d -> p a b d", b=4)[:, :, q, :]
                    nc.vector.scalar_tensor_tensor(
                        out=at, in0=bk_q[q][:, :].rearrange("p (a b) -> p a b", a=M), scalar=1.0 / WSCALE,
                        in1=at, op0=ALU.mult, op1=ALU.add).then_inc(out_ready, 1)

            each_quad(dve, quad)
            rounds(dve, step, combine)
            gated(E * R - 1, R - 1, E - 1)
            combine(R - 1)


def kernel(x, ctx_1024, fside_1x1xSxS2_0, L0_xattn_Wq, L0_xattn_Wk, L0_xattn_Wv, L0_xattn_Wp,
           L0_ffn_gate_w, L0_ffn_w_gate, L0_ffn_w_up, L0_ffn_w_down):
    import numpy as np
    import concourse.bacc as bacc
    from concourse.bass_utils import run_bass_kernel_spmd

    x, context, bias = (np.asarray(a) for a in (x, ctx_1024, fside_1x1xSxS2_0))
    wq, wk, wv, wp = (np.asarray(a) for a in (L0_xattn_Wq, L0_xattn_Wk, L0_xattn_Wv, L0_xattn_Wp))
    gate_w, w_gate, w_up, w_down = (np.asarray(a) for a in (
        L0_ffn_gate_w, L0_ffn_w_gate, L0_ffn_w_up, L0_ffn_w_down))
    d, e, i = x.shape[2], w_gate.shape[0], w_gate.shape[1]
    arrays = {
        "x": x.transpose(1, 0, 2),
        "ctx_t": context.transpose(2, 0, 1),
        "bias": bias[0, 0],
        "wqkv_t": np.concatenate([wq.T, wk.T, wv.T], axis=1),
        "wp_t": wp.T.reshape(-1, 128, d).transpose(1, 0, 2),
        "gate_t": gate_w.T,
        "ffn_w": np.concatenate([
            w_gate.transpose(2, 0, 1).reshape(d, e * i),
            w_up.transpose(2, 0, 1).reshape(d, e * i),
            w_down.transpose(2, 0, 1).reshape(i // 128, 128, e, d).transpose(1, 2, 0, 3).reshape(128, e * i),
        ], axis=1),
    }
    arrays = {name: np.ascontiguousarray(a) for name, a in arrays.items()}
    nc = bacc.Bacc("TRN2", target_bir_lowering=False, num_devices=1)
    args = [nc.dram_tensor(name, a.shape, mybir.dt.from_np(a.dtype), kind="ExternalInput").ap()
            for name, a in arrays.items()]
    out = nc.dram_tensor("out", arrays["x"].shape, F32, kind="ExternalOutput").ap()
    cross_attention_moe_kernel(nc, *args, out)
    got = run_bass_kernel_spmd(nc, [arrays], core_ids=[0])
    return np.ascontiguousarray(got.results[0]["out"].transpose(1, 0, 2))
```

```python
from contextlib import ExitStack

import concourse.bass as bass
from concourse import mybir

ALU = mybir.AluOpType
ACT = mybir.ActivationFunctionType
AX = mybir.AxisListType.X
F32 = mybir.dt.float32
F16 = mybir.dt.float16
U32 = mybir.dt.uint32

EPS = 1e-5
WSCALE = 16.0
FRONT = 5
DRAIN = 3


def cross_attention_moe_kernel(nc, x, ctx_t, bias, wqkv_t, wp_t, gate_t, ffn_w, out):
    S, B, D = x.shape
    K = ctx_t.shape[2]
    HD = wqkv_t.shape[1] // 3
    PAIRS = wp_t.shape[1]
    H = 2 * PAIRS
    DH = HD // H
    GROUPS = 4
    GH = H // GROUPS
    GP = PAIRS // GROUPS
    E = gate_t.shape[1]
    I = ffn_w.shape[1] // (3 * E)
    CAP = S // E * 2
    WCH = ffn_w.shape[1] // B
    SCORE = float(D) ** -0.5 / (WSCALE * WSCALE)
    assert S == 128 and D == 128 and DH == 64 and B % 16 == 0 and CAP == 32

    QK = GP * (S + K)
    OW = DH + 1

    with ExitStack() as ctx:
        def sb(name, shape, dt):
            return ctx.enter_context(nc.sbuf_tensor(name, shape, dt))

        def sem(name):
            return ctx.enter_context(nc.semaphore(name))

        x_sb = sb("x_sb", [S, B, D], F32)
        xg_hi = sb("xg_hi", [S, B, D], F16)
        xg_lo = sb("xg_lo", [S, B, D], F16)
        ffn_hi = sb("ffn_hi", [D, 3 * E * I], F16)
        ffn_lo = sb("ffn_lo", [D, 3 * E * I], F16)
        logits = sb("logits", [S, B, E], F32)
        ident = sb("ident", [128, 128], F32)
        ident_h = sb("ident_h", [128, 128], F16)
        iota = sb("iota", [128, 128], F32)
        gate_sb = sb("gate_sb", [D, E], F32)

        pick = sb("pick", [128, B // 4, 4, E // 4], F32)
        gain = sb("gain", [128, B // 4, E], F32)

        attention(nc, locals())
        routing(nc, locals())
        experts(nc, locals())


def attention(nc, v):
    x, ctx_t, bias, wqkv_t, wp_t, gate_t, ffn_w = (v[n] for n in (
        "x", "ctx_t", "bias", "wqkv_t", "wp_t", "gate_t", "ffn_w"))
    S, B, D, K, HD, H, DH, E = (v[n] for n in ("S", "B", "D", "K", "HD", "H", "DH", "E"))
    PAIRS, GROUPS, GH, GP, WCH, SCORE, QK, OW = (v[n] for n in (
        "PAIRS", "GROUPS", "GH", "GP", "WCH", "SCORE", "QK", "OW"))
    x_sb, xg_hi, xg_lo, ffn_hi, ffn_lo, logits, ident, ident_h, iota, gate_sb = (v[n] for n in (
        "x_sb", "xg_hi", "xg_lo", "ffn_hi", "ffn_lo", "logits", "ident", "ident_h", "iota", "gate_sb"))

    with ExitStack() as ctx:
        def sb(name, shape, dt):
            return ctx.enter_context(nc.sbuf_tensor(name, shape, dt))

        def two(name, shape, dt):
            return [sb(f"{name}{i}", shape, dt) for i in range(2)]

        def bank(name):
            return ctx.enter_context(nc.psum_tensor(name, [128, 512], F32))

        sem = v["sem"]

        w_hi = sb("w_hi", [D, 3 * HD], F16)
        w_lo = sb("w_lo", [D, 3 * HD], F16)
        wp_sb = sb("wp_sb", [2 * DH, PAIRS, D], F32)
        bias_sb = sb("bias_sb", [S, K], F32)
        half = sb("half", [128, 2], F32)
        ctx_f = two("ctx_f", [D, K], F32)
        ctx_hi = two("ctx_hi", [D, K], F16)
        ctx_lo = two("ctx_lo", [D, K], F16)
        wst = two("wst", [D, WCH], F32)
        wsc = sb("wsc", [D, WCH], F32)
        stats = sb("stats", [S, 2, 6], F32)
        mv = sb("mv", [S, 2, 2], F32)
        vpe = sb("vpe", [S, 2], F32)
        rstd = sb("rstd", [S, 2], F32)
        xn = sb("xn", [S, D], F32)
        xn_hi = sb("xn_hi", [S, D], F16)
        xn_lo = sb("xn_lo", [S, D], F16)
        xn2 = sb("xn2", [S, D], F32)
        xT = two("xT", [D, 2, S], F16)
        x2T = sb("x2T", [D, S], F32)
        qk_hi = two("qk_hi", [128, GROUPS, QK], F16)
        qk_lo = two("qk_lo", [128, GROUPS, QK], F16)
        v_hi = two("v_hi", [128, H, OW], F16)
        v_lo = two("v_lo", [128, H, DH], F16)
        v_f = two("v_f", [128, GH, DH], F32)
        neg = two("neg", [S, GH, K], F32)
        negmax = two("negmax", [S, GH], F32)
        probs = two("probs", [S, GH, K], F32)
        pT_hi = two("pT_hi", [128, GH, S], F16)
        pT_lo = two("pT_lo", [128, GH, S], F16)
        rsum = sb("rsum", [S, GH], F32)
        o_sb = two("o_sb", [S, GH, DH], F32)
        oT = two("oT", [2 * DH, GP, S], F32)
        w_f = sb("w_f", [D, 3 * HD], F32)

        bk_s = [bank("bk_s0"), bank("bk_s1")]
        bk_t, bk_a, bk_b, bk_o, bk_x, bk_y = (bank(n) for n in (
            "bk_t", "bk_a", "bk_b", "bk_o", "bk_x", "bk_y"))

        loaded_w, loaded_b, loaded = sem("loaded_w"), sem("loaded_b"), sem("loaded")
        const_ready = sem("const_ready")
        ident_h_ready = sem("ident_h_ready")
        w_hi_ready, w_ready = sem("w_hi_ready"), sem("w_ready")
        bias_ready = sem("bias_ready")
        ctx_ready, ffnw_ready = sem("ctx_ready"), sem("ffnw_ready")
        pool_chain, dve_chain = sem("pool_chain"), sem("dve_chain")
        stats_ready, rstd_ready = sem("stats_ready"), sem("rstd_ready")
        xn_ready, xn2_ready = sem("xn_ready"), sem("xn2_ready")
        xg_ready = sem("xg_ready")
        xT_written, x2T_written = sem("xT_written"), sem("x2T_written")
        xn_parts_ready, xT_ready, x2T_ready = sem("xn_parts_ready"), sem("xT_ready"), sem("x2T_ready")
        qk_written, qk_hi_ready, qk_lo_ready = sem("qk_written"), sem("qk_hi_ready"), sem("qk_lo_ready")
        v_written, v_hi_ready, v_lo_ready = sem("v_written"), sem("v_hi_ready"), sem("v_lo_ready")
        scores_written, neg_ready, probs_ready = sem("scores_written"), sem("neg_ready"), sem("probs_ready")
        pT_written, pT_hi_ready, pT_lo_ready = sem("pT_written"), sem("pT_hi_ready"), sem("pT_lo_ready")
        pv_written, o_ready = sem("pv_written"), sem("o_ready")
        oT_written, oT_ready = sem("oT_written"), sem("oT_ready")
        proj_written, x1_ready = sem("proj_written"), sem("x1_ready")
        logits_written, logits_ready = sem("logits_written"), sem("logits_ready")

        first, last = -1, B + DRAIN
        loop_end = B - 1
        assert (loop_end - FRONT) % 2 == 0

        def live(b):
            return not isinstance(b, int) or 0 <= b < B

        def upto(count):
            return min(count, B) if isinstance(count, int) else count

        def some(count):
            return not isinstance(count, int) or count > 0

        def alone(eng):
            eng.nop(nofuse=True)

        def slots(eng, slot, end=last, loop_end=loop_end, first=first):
            for t in range(first, FRONT):
                slot(t, t % 2)
            with eng.Fori(FRONT, loop_end - 1, 2) as t:
                slot(t, FRONT % 2)
                slot(t + 1, (FRONT + 1) % 2)
            for t in range(loop_end, end):
                slot(t, t % 2)

        def behind(t, g, k):
            return t - 1 + (g - k) // GROUPS, (g - k) % GROUPS

        block = ctx.enter_context(nc.Block())

        @block.sync
        def _(sp):
            def slot(t, par):
                if some(t * 48):
                    sp.wait_ge(loaded, t * 48)
                sp.dma_start(x_sb[:, t, :], x[:, t, :]).then_inc(loaded, 16)
                if some(t - 1):
                    sp.wait_ge(ctx_ready, t - 1)
                sp.dma_start(ctx_f[par][:, :], ctx_t[:, t, :]).then_inc(loaded, 16)
                if some(t - 1):
                    sp.wait_ge(ffnw_ready, t - 1)
                src = ffn_w[:, bass.ds(t * WCH, WCH)] if not isinstance(t, int) else ffn_w[:, t * WCH:(t + 1) * WCH]
                sp.dma_start(wst[par][:, :], src).then_inc(loaded, 16)

            slots(sp, slot, end=B, first=0)

        @block.gpsimd
        def _(pool):
            pool.memset(ident[:, :], 0.0).then_inc(pool_chain, 1)
            pool.memset(half[:, :], -0.5).then_inc(const_ready, 1)
            pool.memset(vpe[:, :], 1.0).then_inc(const_ready, 1)
            pool.memset(mv[:, :, :], 1.0).then_inc(const_ready, 1)
            for i in range(2):
                pool.memset(v_hi[i][:, :, DH:OW], 1.0).then_inc(const_ready, 1)
            pool.wait_ge(pool_chain, 1)
            pool.affine_select(out=ident[:, :], in_=ident[:, :], compare_op=ALU.not_equal, fill=1.0,
                               base=0, pattern=[[-1, 128]], channel_multiplier=1).then_inc(const_ready, 1)
            pool.iota(iota[:, :], pattern=[[1, 128]], base=0, channel_multiplier=0,
                      allow_small_or_imprecise_dtypes=True).then_inc(const_ready, 1)
            pool.wait_ge(const_ready, 7)
            pool.tensor_copy(ident_h[:, :], ident[:, :]).then_inc(ident_h_ready, 1)

            def values(t, g, par):
                if live(t):
                    pool.wait_ge(v_hi_ready, 4 * t + g + 1)
                    if some(4 * (t - 2) + g + 1):
                        pool.wait_ge(pv_written, 4 * (t - 2) + g + 1)
                    pool.tensor_tensor(v_lo[par][0:K, GH * g:GH * (g + 1), :], v_f[g % 2][0:K, :, :],
                                       v_hi[par][0:K, GH * g:GH * (g + 1), 0:DH], ALU.subtract).then_inc(v_lo_ready, 1)

            def slot(t, par):
                c = chain(t)
                at = slice(t * WCH, (t + 1) * WCH) if isinstance(t, int) else bass.ds(t * WCH, WCH)
                i = (par + 1) % 2
                values(t - 1, GROUPS - 1, i)
                pool.wait_ge(stats_ready, t + 2)
                alone(pool)
                pool.tensor_scalar(vpe[:, :], mv[:, :, 1], EPS, None, ALU.add).then_inc(pool_chain, 1)
                pool.wait_ge(pool_chain, c[0])
                if some(upto(t + 1)):
                    pool.wait_ge(xn_ready, upto(t + 1))
                if some(t - 3):
                    pool.wait_ge(xn2_ready, t - 3)
                pool.tensor_tensor(rstd[:, :], vpe[:, :], half[:, :], ALU.pow).then_inc(rstd_ready, 1)
                if live(t + 1):
                    pool.wait_ge(loaded, (t + 2) * 48)
                    if some(4 * t):
                        pool.wait_ge(v_written, 4 * t)
                    alone(pool)
                    pool.tensor_copy(ctx_hi[i][:, :], ctx_f[i][:, :]).then_inc(pool_chain, 1)
                if live(t):
                    if some(t):
                        pool.wait_ge(ffnw_ready, t)
                    alone(pool)
                    pool.tensor_scalar(wsc[:, :], wst[par][:, :], WSCALE, None, ALU.mult).then_inc(pool_chain, 1)
                values(t, 0, par)
                if live(t + 1):
                    pool.wait_ge(pool_chain, c[1])
                    pool.tensor_tensor(ctx_lo[i][:, :], ctx_f[i][:, :], ctx_hi[i][:, :],
                                       ALU.subtract).then_inc(ctx_ready, 1)
                    pool.wait_ge(xn_ready, t + 2)
                    if some(t + 1):
                        pool.wait_ge(xT_written, t + 1)
                    alone(pool)
                    pool.tensor_copy(xn_hi[:, :], xn[:, :]).then_inc(pool_chain, 1)
                    pool.wait_ge(pool_chain, c[3])
                    pool.tensor_tensor(xn_lo[:, :], xn[:, :], xn_hi[:, :], ALU.subtract).then_inc(xn_parts_ready, 1)
                values(t, 1, par)
                if live(t):
                    pool.wait_ge(pool_chain, c[2])
                    alone(pool)
                    pool.tensor_copy(ffn_hi[:, at], wsc[:, :]).then_inc(pool_chain, 1)
                if live(t - 3):
                    pool.wait_ge(xn2_ready, t - 2)
                    alone(pool)
                    pool.tensor_copy(xg_hi[:, t - 3, :], xn2[:, :]).then_inc(pool_chain, 1)
                values(t, 2, par)
                if live(t):
                    pool.wait_ge(pool_chain, c[4])
                    pool.tensor_tensor(ffn_lo[:, at], wsc[:, :], ffn_hi[:, at], ALU.subtract).then_inc(ffnw_ready, 1)
                if live(t - 3):
                    pool.wait_ge(pool_chain, c[5])
                    pool.tensor_tensor(xg_lo[:, t - 3, :], xn2[:, :], xg_hi[:, t - 3, :],
                                       ALU.subtract).then_inc(xg_ready, 1)

            def chain(t):
                def before(lag, each):
                    return each * (t - lag) if not isinstance(t, int) else each * min(max(t - lag, 0), B)
                c = 1 + (t + 1) + before(-1, 2) + before(0, 2) + before(3, 1)
                out = [c + 1]
                for batch in (t + 1, t, t + 1, t, t - 3):
                    out.append(out[-1] + (1 if live(batch) else 0))
                return out

            slots(pool, slot)

        @block.scalar
        def _(act):
            act.dma_start(w_f[:, :], wqkv_t).then_inc(loaded_w, 16)
            act.dma_start(bias_sb[:, :], bias).then_inc(loaded_b, 16)
            act.dma_start(wp_sb[:, :, :], wp_t).then_inc(loaded_b, 16)
            act.dma_start(gate_sb[:, :], gate_t).then_inc(loaded_b, 16)
            act.wait_ge(loaded_w, 16)
            nc.scalar.activation(w_hi[:, :], w_f[:, :], ACT.Copy, scale=WSCALE).then_inc(w_hi_ready, 1)

            def step(t, par, g):
                n = 4 * (t - 1) + g
                tw, gw, pw = (t, g - 1, par) if g else (t - 1, GROUPS - 1, (par + 1) % 2)
                b4, g4 = behind(t, g, 4)
                if live(b4):
                    act.wait_ge(oT_written, 4 * b4 + g4 + 1)
                    if some(4 * b4 + g4 - 1):
                        act.wait_ge(proj_written, 4 * b4 + g4 - 1)
                    nc.scalar.copy(oT[g4 % 2][:, :, :].rearrange("p a b -> p (a b)"),
                                   bk_x[:, 0:GP * S]).then_inc(oT_ready, 1)
                if gw == 2 and live(tw - 3):
                    act.wait_ge(x2T_written, tw - 2)
                    if live(b4):
                        act.wait_ge(oT_written, 4 * b4 + g4 + 1)
                    if some(tw - 3):
                        act.wait_ge(logits_written, tw - 3)
                    nc.scalar.copy(x2T[:, :], bk_x[:, 384:512]).then_inc(x2T_ready, 1)
                if live(tw):
                    act.wait_ge(qk_written, 4 * tw + gw + 1)
                    if some(4 * (tw - 2) + gw + 1):
                        act.wait_ge(scores_written, 4 * (tw - 2) + gw + 1)
                    nc.scalar.copy(qk_hi[pw][:, gw, :], bk_a[:, 0:QK]).then_inc(qk_hi_ready, 1)
                if gw == GROUPS - 1 and live(tw - 3):
                    act.wait_ge(logits_written, tw - 2)
                    if live(tw):
                        act.wait_ge(v_written, 4 * tw + gw + 1)
                    nc.scalar.copy(logits[:, tw - 3, :], bk_b[:, 256:256 + E]).then_inc(logits_ready, 1)
                if live(tw):
                    act.wait_ge(v_written, 4 * tw + gw + 1)
                    if some(4 * tw + gw - 1):
                        act.wait_ge(v_lo_ready, 4 * tw + gw - 1)
                    values = bk_b[0:K, 0:GH * DH].rearrange("p (a b) -> p a b", a=GH)
                    nc.scalar.copy(v_f[gw % 2][0:K, :, :], values)
                    if some(4 * (tw - 2) + gw + 1):
                        act.wait_ge(pv_written, 4 * (tw - 2) + gw + 1)
                    nc.scalar.copy(v_hi[pw][0:K, GH * gw:GH * (gw + 1), 0:DH], values).then_inc(v_hi_ready, 1)
                b1, g1 = behind(t, g, 1)
                if live(b1):
                    act.wait_ge(pT_written, 4 * b1 + g1 + 1)
                    if some(4 * b1 + g1 - 1):
                        act.wait_ge(pv_written, 4 * b1 + g1 - 1)
                    nc.scalar.copy(pT_hi[g1 % 2][0:K, :, :].rearrange("p a b -> p (a b)"),
                                   bk_t[0:K, :]).then_inc(pT_hi_ready, 1)
                if gw == 2 and live(tw + 1):
                    act.wait_ge(xT_written, tw + 2)
                    if some(4 * tw):
                        act.wait_ge(qk_written, 4 * tw)
                    nc.scalar.copy(xT[(pw + 1) % 2][:, :, :].rearrange("p a b -> p (a b)"),
                                   bk_x[:, 256:384].bitcast(F16)).then_inc(xT_ready, 1)
                if live(t - 1):
                    act.wait_ge(neg_ready, n + 1)
                    if some(n - 1):
                        act.wait_ge(pT_written, n - 1)
                    for i in range(GH):
                        e = nc.scalar.activation(probs[g % 2][:, i, :], neg[g % 2][:, i, :], ACT.Exp,
                                                 bias=negmax[g % 2][:, i:i + 1], scale=-1.0)
                    e.then_inc(probs_ready, 1)

            slots(act, lambda t, par: [step(t, par, g) for g in range(GROUPS)])
            step(last, last % 2, 0)

        @block.vector
        def _(dve):
            dve.wait_ge(loaded_b, 48)
            nc.vector.tensor_scalar(bias_sb[:, :], bias_sb[:, :], 1.0 / SCORE, None,
                                    ALU.mult).then_inc(bias_ready, 1)
            dve.wait_ge(w_hi_ready, 1)
            nc.vector.scalar_tensor_tensor(out=w_lo[:, :], in0=w_f[:, :], scalar=WSCALE, in1=w_hi[:, :],
                                           op0=ALU.mult, op1=ALU.subtract).then_inc(w_ready, 1)
            dve.wait_ge(bias_ready, 1)
            dve.wait_ge(const_ready, 7)

            def chain(t):
                if not isinstance(t, int):
                    return (t + 1) + (t - 3) + 4 * (t - 1) - 2
                part = lambda lag: min(max(t - lag, 0), B)
                return part(-1) + part(3) + max(min(4 * (t - 1) - 2, 4 * B), 0)

            def step(t, par, g, c):
                n = 4 * (t - 1) + g
                tw, gw, pw = (t, g - 1, par) if g else (t - 1, GROUPS - 1, (par + 1) % 2)
                if g == 0 and live(t - 3):
                    dve.wait_ge(proj_written, 4 * (t - 3) + 4)
                    nc.vector.tensor_tensor(x_sb[:, t - 3, :], x_sb[:, t - 3, :], bk_y[:, 0:D],
                                            ALU.add).then_inc(x1_ready, 1)
                if live(t - 1):
                    dve.wait_ge(scores_written, n + 1)
                    if some(n - 1):
                        dve.wait_ge(probs_ready, n - 1)
                    alone(dve)
                    for i in range(GH):
                        r = nc.vector.tensor_tensor_reduce(
                            out=neg[g % 2][:, i, :], in0=bk_s[i % 2][:, (i // 2) * K:(i // 2 + 1) * K],
                            in1=bias_sb[:, :], scale=-SCORE, scalar=3.0e38, op0=ALU.add, op1=ALU.min,
                            accum_out=negmax[g % 2][:, i:i + 1])
                    r.then_inc(neg_ready, 1)
                if live(tw):
                    dve.wait_ge(qk_hi_ready, 4 * tw + gw + 1)
                    if some(4 * (tw - 2) + gw + 1):
                        dve.wait_ge(scores_written, 4 * (tw - 2) + gw + 1)
                    nc.vector.tensor_tensor(qk_lo[pw][:, gw, :], bk_a[:, 0:QK], qk_hi[pw][:, gw, :],
                                            ALU.subtract).then_inc(qk_lo_ready, 1)
                if g == 0 and live(t - 3):
                    dve.wait_ge(x1_ready, t - 2)
                    alone(dve)
                    nc.vector.bn_stats(stats[:, 1, :], x_sb[:, t - 3, :]).then_inc(dve_chain, 1)
                    c = c + 1
                if g == 0 and live(t + 1):
                    dve.wait_ge(loaded, (t + 2) * 48)
                    alone(dve)
                    nc.vector.bn_stats(stats[:, 0, :], x_sb[:, t + 1, :]).then_inc(dve_chain, 1)
                    c = c + 1
                stats_count = c
                b2, g2 = behind(t, g, 2)
                if live(b2):
                    dve.wait_ge(pv_written, 4 * b2 + g2 + 1)
                    o = bk_o[:, 0:GH * OW].rearrange("p (a b) -> p a b", a=GH)
                    nc.vector.reciprocal(rsum[:, :], o[:, :, DH]).then_inc(dve_chain, 1)
                    c = c + 1
                if g == 0:
                    if some(stats_count):
                        dve.wait_ge(dve_chain, stats_count)
                    if some(t + 1):
                        dve.wait_ge(rstd_ready, t + 1)
                    alone(dve)
                    for k in [k for k, b in ((0, t + 1), (1, t - 3)) if live(b)]:
                        a = nc.vector.bn_aggr(mv[:, k, :], stats[:, k, :])
                    a.then_inc(stats_ready, 1)
                b1, g1 = behind(t, g, 1)
                if live(b1):
                    dve.wait_ge(pT_hi_ready, 4 * b1 + g1 + 1)
                    if some(4 * b1 + g1 - 1):
                        dve.wait_ge(pv_written, 4 * b1 + g1 - 1)
                    nc.vector.tensor_tensor(pT_lo[g1 % 2][0:K, :, :].rearrange("p a b -> p (a b)"), bk_t[0:K, :],
                                            pT_hi[g1 % 2][0:K, :, :].rearrange("p a b -> p (a b)"),
                                            ALU.subtract).then_inc(pT_lo_ready, 1)
                if live(b2):
                    dve.wait_ge(dve_chain, c)
                    if some(4 * b2 + g2 - 1):
                        dve.wait_ge(oT_written, 4 * b2 + g2 - 1)
                    nc.vector.scalar_tensor_tensor(
                        out=o_sb[g2 % 2][:, :, :], in0=o[:, :, 0:DH], scalar=1.0 / WSCALE,
                        in1=rsum[:, :].rearrange("p (a b) -> p a b", b=1).to_broadcast([S, GH, DH]),
                        op0=ALU.mult, op1=ALU.mult).then_inc(o_ready, 1)
                if g == 1:
                    dve.wait_ge(rstd_ready, t + 2)
                    if live(t + 1):
                        if some(t + 1):
                            dve.wait_ge(xn_parts_ready, t + 1)
                        nc.vector.tensor_scalar(xn[:, :], x_sb[:, t + 1, :], mv[:, 0, 0:1], rstd[:, 0:1],
                                                ALU.subtract, ALU.mult).then_inc(xn_ready, 1)
                    if live(t - 3):
                        if some(t - 3):
                            dve.wait_ge(x2T_written, t - 3)
                        if some(t - 3):
                            dve.wait_ge(xg_ready, t - 3)
                        nc.vector.tensor_scalar(xn2[:, :], x_sb[:, t - 3, :], mv[:, 1, 0:1], rstd[:, 1:2],
                                                ALU.subtract, ALU.mult).then_inc(xn2_ready, 1)
                return c

            def slot(t, par):
                c = chain(t)
                for g in range(GROUPS):
                    c = step(t, par, g, c)

            slots(dve, slot)

        @block.tensor
        def _(pe):
            pe.wait_ge(const_ready, 7)
            pe.wait_ge(ident_h_ready, 1)
            pe.wait_ge(loaded_b, 48)

            def product(out, lhs, rhs, **kw):
                (lh, ll), (rh, rl) = lhs, rhs
                nc.tensor.matmul(out, lh, rh, start=True, stop=False)
                nc.tensor.matmul(out, ll, rh, start=False, stop=False)
                return nc.tensor.matmul(out, lh, rl, start=False, stop=True)

            def step(t, par, g):
                n = 4 * (t - 1) + g
                if live(t - 1):
                    p1 = (par + 1) % 2
                    pe.wait_ge(qk_lo_ready, n + 1)
                    if some(n):
                        pe.wait_ge(neg_ready, n)
                    for j in range(GP):
                        for lo_q, lo_k in ((0, 0), (1, 0), (0, 1)):
                            for h in range(2):
                                r = slice(DH * h, DH * (h + 1))
                                q = (qk_hi, qk_lo)[lo_q][p1][r, g, j * S:(j + 1) * S]
                                k = (qk_hi, qk_lo)[lo_k][p1][r, g, GP * S + j * K:GP * S + (j + 1) * K]
                                m = nc.tensor.matmul(bk_s[h][:, j * K:(j + 1) * K], q, k,
                                                     start=lo_q + lo_k == 0, stop=lo_k == 1)
                    m.then_inc(scores_written, 1)
                b1, g1 = behind(t, g, 1)
                if live(b1):
                    pe.wait_ge(probs_ready, 4 * b1 + g1 + 1)
                    if some(4 * b1 + g1):
                        pe.wait_ge(pT_lo_ready, 4 * b1 + g1)
                    for i in range(GH):
                        m = nc.tensor.transpose(bk_t[0:K, i * S:(i + 1) * S], probs[g1 % 2][:, i, :], ident[:, :])
                    m.then_inc(pT_written, 1)
                b2, g2 = behind(t, g, 2)
                if live(b2):
                    p2 = (par + 1) % 2 if g >= 2 else par
                    pe.wait_ge(pT_lo_ready, 4 * b2 + g2 + 1)
                    pe.wait_ge(v_lo_ready, 4 * b2 + g2 + 1)
                    if some(4 * b2 + g2):
                        pe.wait_ge(o_ready, 4 * b2 + g2)
                    for i in range(GH):
                        h = GH * g2 + i
                        ph, pl = pT_hi[g2 % 2][0:K, i, :], pT_lo[g2 % 2][0:K, i, :]
                        nc.tensor.matmul(bk_o[:, i * OW:(i + 1) * OW], ph, v_hi[p2][0:K, h, :], start=True, stop=False)
                        nc.tensor.matmul(bk_o[:, i * OW:i * OW + DH], ph, v_lo[p2][0:K, h, :], start=False, stop=False)
                        m = nc.tensor.matmul(bk_o[:, i * OW:(i + 1) * OW], pl, v_hi[p2][0:K, h, :], start=False, stop=True)
                    m.then_inc(pv_written, 1)
                if g == 0:
                    if some(upto(t - 3)):
                        pe.wait_ge(logits_ready, upto(t - 3))
                if live(t):
                    if some(4 * t + g):
                        pe.wait_ge(v_hi_ready, 4 * t + g)
                if g == GROUPS - 1 and live(t - 3):
                    pe.wait_ge(x2T_ready, t - 2)
                    nc.tensor.matmul(bk_b[:, 256:256 + E], x2T[:, :], gate_sb[:, :],
                                     start=True, stop=True).then_inc(logits_written, 1)
                if live(t):
                    if g == 0:
                        if some(1):
                            pe.wait_ge(w_ready, 1)
                        pe.wait_ge(ctx_ready, t + 1)
                    cT = ctx_hi[par][:, :], ctx_lo[par][:, :]
                    c = 2 * HD + GH * DH * g
                    product(bk_b[0:K, 0:GH * DH], cT, (w_hi[:, c:c + GH * DH], w_lo[:, c:c + GH * DH])
                            ).then_inc(v_written, 1)
                b3, g3 = behind(t, g, 3)
                if live(b3) or g == 2:
                    if live(b3) and some(4 * b3 + g3):
                        pe.wait_ge(oT_ready, 4 * b3 + g3)
                    if g == 3:
                        if live(t + 1) and some(t + 2):
                            pe.wait_ge(xT_ready, t + 2)
                        if live(t - 3) and some(t - 2):
                            pe.wait_ge(x2T_ready, t - 2)
                    if g == 2:
                        if live(t) and some(t + 1):
                            pe.wait_ge(xT_ready, t + 1)
                        if live(t - 3) and some(t - 3):
                            pe.wait_ge(x2T_ready, t - 3)
                        if live(t + 1):
                            pe.wait_ge(xn_parts_ready, t + 2)
                            parts = bk_x[:, 256:384].bitcast(F16)
                            nc.tensor.transpose(parts[:, 0:S], xn_hi[:, :], ident_h[:, :])
                            nc.tensor.transpose(parts[:, S:2 * S], xn_lo[:, :], ident_h[:, :]).then_inc(xT_written, 1)
                        if live(t - 3):
                            pe.wait_ge(xn2_ready, t - 2)
                            nc.tensor.transpose(bk_x[:, 384:512], xn2[:, :], ident[:, :]).then_inc(x2T_written, 1)
                if live(b3):
                    pe.wait_ge(o_ready, 4 * b3 + g3 + 1)
                    for j in range(GP):
                        m = nc.tensor.transpose(bk_x[:, j * S:(j + 1) * S],
                                                o_sb[g3 % 2][:, 2 * j:2 * j + 2, :].rearrange("p a b -> p (a b)"),
                                                ident[:, :])
                    m.then_inc(oT_written, 1)
                b4, g4 = behind(t, g, 4)
                if live(b4):
                    pe.wait_ge(oT_ready, 4 * b4 + g4 + 1)
                    if g4 == 0:
                        if some(b4):
                            pe.wait_ge(x1_ready, b4)
                    for j in range(GP):
                        m = nc.tensor.matmul(bk_y[:, 0:D], oT[g4 % 2][:, j, :], wp_sb[:, GP * g4 + j, :],
                                             start=(g4 == 0 and j == 0), stop=(g4 == GROUPS - 1 and j == GP - 1))
                    m.then_inc(proj_written, 1)

                if live(t):
                    if g == 0:
                        pe.wait_ge(xT_ready, t + 1)
                    if some(4 * t + g):
                        pe.wait_ge(qk_lo_ready, 4 * t + g)
                    xp = xT[par][:, 0, :], xT[par][:, 1, :]
                    for j in range(GP):
                        for base, at, wide, r in ((0, j * S, S, xp), (HD, GP * S + j * K, K, cT)):
                            c = base + 2 * DH * (GP * g + j)
                            w = w_hi[:, c:c + 2 * DH], w_lo[:, c:c + 2 * DH]
                            m = product(bk_a[:, at:at + wide], w, r)
                    m.then_inc(qk_written, 1)

            slots(pe, lambda t, par: [step(t, par, g) for g in range(GROUPS)])


def routing(nc, v):
    S, B, E, CAP, WSCALE_ = v["S"], v["B"], v["E"], v["CAP"], WSCALE
    logits, ident, pick, gain, sem = (v[n] for n in ("logits", "ident", "pick", "gain", "sem"))
    R = B // 16

    with ExitStack() as ctx:
        def sb(name, shape, dt):
            return ctx.enter_context(nc.sbuf_tensor(name, shape, dt))

        top = sb("top", [S, B], F32)
        shifted = sb("shifted", [S, B, E], F32)
        weights = sb("weights", [S, B, E], F32)
        total = sb("total", [S, B], F32)
        share = sb("share", [S, B], F32)
        aff = sb("aff", [S, R, 4, 4, E], F32)
        affT = sb("affT", [128, R, S], F32)
        vals = sb("vals", [128, R, CAP], F32)
        idx = sb("idx", [128, R, CAP], U32)
        idx_f = sb("idx_f", [128, R, CAP], F32)
        vals_T = sb("vals_T", [128, R, CAP], F32)
        regroup = sb("regroup", [128, 4, 4, 4, E // 4], F32)
        idx_g = sb("idx_g", [128, R, CAP], F32)
        bk_idx = ctx.enter_context(nc.psum_tensor("bk_idx", [128, R, CAP], F32))
        bk_aff = ctx.enter_context(nc.psum_tensor("bk_aff", [128, R, S], F32))
        exp_ready, aff_ready, aff_written, chain = (sem(n) for n in (
            "exp_ready", "aff_ready", "aff_written", "routing_chain"))
        shifted_ready = sem("shifted_ready")
        idx_ready, idx_written = sem("idx_ready"), sem("idx_written")

        block = ctx.enter_context(nc.Block())

        @block.scalar
        def _(act):
            act.wait_ge(shifted_ready, 1)
            nc.scalar.activation(weights[:, :, :], shifted[:, :, :], ACT.Exp).then_inc(exp_ready, 1)

        @block.tensor
        def _(pe):
            pe.wait_ge(aff_ready, 1)
            for r in range(R):
                m = nc.tensor.transpose(bk_aff[:, r, :], aff[:, r, :, :, :].rearrange("p a b c -> p (a b c)"),
                                        ident[:, :])
            m.then_inc(aff_written, 1)
            pe.wait_ge(idx_ready, 1)
            nc.tensor.matmul(bk_idx[:, :, :].rearrange("p a b -> p (a b)"),
                             regroup[:, :, :, :, :].rearrange("p a b c d -> p (a b c d)"),
                             idx_f[:, :, :].rearrange("p a b -> p (a b)"), start=True, stop=True
                             ).then_inc(idx_written, 1)

        @block.vector
        def _(dve):
            count = [0]

            def done(instruction):
                count[0] += 1
                instruction.then_inc(chain, 1)
                dve.wait_ge(chain, count[0])

            def over_experts(a):
                return a.rearrange("p (a b) -> p a b", b=1).to_broadcast([S, B, E])

            columns = ident[:, :].rearrange("p (q j c g) -> p q j c g", q=4, j=4, c=E // 4)
            for j in range(4):
                for c in range(E // 4):
                    nc.vector.tensor_copy(regroup[:, :, j, :, c], columns[:, :, j, c, :].rearrange("p q g -> p g q"))
            done(nc.vector.tensor_reduce(top[:, :], logits[:, :, :], AX, ALU.max))
            nc.vector.tensor_tensor(shifted[:, :, :], logits[:, :, :], over_experts(top[:, :]),
                                    ALU.subtract).then_inc(shifted_ready, 1)
            dve.wait_ge(exp_ready, 1)
            done(nc.vector.tensor_reduce(total[:, :], weights[:, :, :], AX, ALU.add))
            done(nc.vector.reciprocal(share[:, :], total[:, :]))
            for r in range(R):
                at = slice(16 * r, 16 * (r + 1))
                a = nc.vector.tensor_tensor(
                    aff[:, r, :, :, :].rearrange("p q j e -> p j q e"),
                    weights[:, at, :].rearrange("p (j q) e -> p j q e", j=4),
                    share[:, at].rearrange("p (j q c) -> p j q c", j=4, c=1).to_broadcast([S, 4, 4, E]), ALU.mult)
            a.then_inc(aff_ready, 1)
            dve.wait_ge(aff_written, 1)
            done(nc.vector.tensor_copy(affT[:, :, :], bk_aff[:, :, :]))
            for k in range(CAP // 8):
                at = slice(8 * k, 8 * (k + 1))
                for r in range(R):
                    m = nc.vector.max(vals[:, r, at], affT[:, r, :])
                done(m)
                for r in range(R):
                    m = nc.vector.max_index(idx[:, r, at], vals[:, r, at], affT[:, r, :])
                done(m)
                for r in range(R):
                    m = nc.vector.match_replace(out=affT[:, r, :], in_to_replace=vals[:, r, at],
                                                in_values=affT[:, r, :], imm_value=-1.0)
                done(m)
            nc.vector.tensor_copy(idx_f[:, :, :], idx[:, :, :]).then_inc(idx_ready, 1)
            flat = lambda a: a.rearrange("p a b -> p (a b)")
            done(nc.vector.transpose(flat(vals_T[:, :, :]), flat(vals[:, :, :])))
            done(nc.vector.tensor_scalar(flat(gain[:, :, :]), flat(vals_T[:, :, :]), 1.0 / WSCALE, None, ALU.mult))
            dve.wait_ge(idx_written, 1)
            done(nc.vector.tensor_copy(idx_g[:, :, :], bk_idx[:, :, :]))
            done(nc.vector.transpose(pick[:, :, :, :].rearrange("p a b c -> p (a b c)"), flat(idx_g[:, :, :])))


def experts(nc, v):
    S, B, D, E, I, CAP = (v[n] for n in ("S", "B", "D", "E", "I", "CAP"))
    x_sb, xg_hi, xg_lo, ffn_hi, ffn_lo, ident_h, iota, pick, gain, out, sem = (v[n] for n in (
        "x_sb", "xg_hi", "xg_lo", "ffn_hi", "ffn_lo", "ident_h", "iota", "pick", "gain", "out", "sem"))
    R = B // 16
    M = 4
    T = M * 4 * CAP
    IC = I // 128
    UP, DOWN = E * I, 2 * E * I

    with ExitStack() as ctx:
        def sb(name, shape, dt):
            return ctx.enter_context(nc.sbuf_tensor(name, shape, dt))

        def two(name, shape, dt):
            return [sb(f"{name}{i}", shape, dt) for i in range(2)]

        def bank(name, dt=F32):
            return ctx.enter_context(nc.psum_tensor(name, [128, 2048 // mybir.dt.size(dt)], dt))

        x_in = sb("x_in", [D, 2, 2, E, T], F16)
        hid = [[sb(f"hid{i}{j}", [128, IC, T], F16) for j in range(2)] for i in range(2)]
        silu = two("silu", [128, T], F32)
        hid_f = two("hid_f", [128, T], F32)
        y_f = sb("y_f", [128, T], F32)
        y = sb("y", [128, 2, M, D], F16)
        y_all = sb("y_all", [128, E // 4, 4, 2, M, D], F16)
        hot_t = sb("hot_t", [128, 4 * (E // 4), S], F16)
        hot = sb("hot", [S, 4 * (E // 4), 128], F16)
        back = sb("back", [128, M, 4 * (E // 4), S], F16)
        bk_g, bk_u = [bank("bk_g0"), bank("bk_g1")], [bank("bk_u0"), bank("bk_u1")]
        bk_y, bk_c, bk_x = bank("bk_y2"), bank("bk_c"), bank("bk_x2")
        bk_h = bank("bk_h", F16)
        gate_written, up_written, down_written = sem("gate_written"), sem("up_written"), sem("down_written")
        silu_ready, hid_f_ready = sem("silu_ready"), sem("hid_f_ready")
        hid_hi_ready, hid_lo_ready = sem("hid_hi_ready"), sem("hid_lo_ready")
        y_f_ready, y_hi_ready, y_lo_ready = sem("y_f_ready"), sem("y_hi_ready"), sem("y_lo_ready")
        hot_t_ready, hot_written, hot_ready = sem("hot_t_ready"), sem("hot_written"), sem("hot_ready")
        gather_written, x_in_ready = sem("gather_written"), sem("x_in_ready")
        back_ready, scatter_written, out_ready = sem("back_ready"), sem("scatter_written"), sem("out_ready")
        y_moved, stored = sem("y_moved"), sem("stored")

        def some(count):
            return not isinstance(count, int) or count > 0

        def each_quad(eng, quad):
            quad(0)
            with eng.Fori(1, M, 1) as m:
                quad(m)

        def rounds(eng, step):
            def one(r, gather, scatter):
                step(r, 0, 0, gather, False)
                step(r, 1, 1, gather, scatter)
                with eng.Fori(2, E - 1, 2) as e:
                    step(r, e, 0, gather, False)
                    step(r, e + 1, 1, gather, False)

            one(0, R > 1, False)
            if R > 2:
                with eng.Fori(1, R - 1, 1) as r:
                    one(r, True, True)
            if R > 1:
                one(R - 1, False, True)

        def quad_of(e, odd):
            if isinstance(e, int):
                return e // 2
            return (e - odd) // 2

        block = ctx.enter_context(nc.Block())

        @block.sync
        def _(sp):
            def move(r, e):
                sp.wait_ge(y_lo_ready, E * r + e + 1)
                sp.nop(nofuse=True)
                if e == 0:
                    if some(M * r):
                        sp.wait_ge(scatter_written, M * r)
                to = slice(CAP * (e % 4), CAP * (e % 4 + 1))
                for q in range(4):
                    sp.dma_start(y_all[to, e // 4, q, :, :, :], y[CAP * q:CAP * (q + 1), :, :, :]).then_inc(y_moved, 16)

            def store(r, m):
                sp.wait_ge(out_ready, M * r + m + 1)
                sp.nop(nofuse=True)
                b = 16 * r + 4 * m
                at = bass.ds(b, 4) if not isinstance(b, int) else slice(b, b + 4)
                sp.dma_start(out[:, at, :], x_sb[:, at, :]).then_inc(stored, 16)

            def one(r, stores):
                for e in range(E):
                    if stores and e < M:
                        store(r - 1, e)
                    move(r, e)

            one(0, False)
            with sp.Fori(1, R, 1) as r:
                one(r, True)
            for m in range(M):
                store(R - 1, m)
            sp.wait_ge(stored, 16 * R * M)

        @block.tensor
        def _(pe):
            def turn(r1, m):
                a = 4 * r1 + m
                pe.wait_ge(hot_t_ready, a + 1)
                if some(a):
                    pe.wait_ge(hot_ready, a)
                for i in range(E):
                    t = nc.tensor.transpose(bk_h[:, i * 128:(i + 1) * 128], hot_t[:, i, :], ident_h[:, :])
                t.then_inc(hot_written, 1)

            def gather(r1, m, q):
                a = 4 * (4 * r1 + m) + q
                pe.wait_ge(hot_ready, 4 * r1 + m + 1)
                if some(a):
                    pe.wait_ge(x_in_ready, a)
                G = E // 4
                rhs = hot[:, G * q:G * (q + 1), :].rearrange("p a b -> p (a b)")
                b = 16 * r1 + 4 * m + q
                nc.tensor.matmul(bk_x[:, 0:E * CAP], xg_hi[:, b, :], rhs, start=True, stop=True)
                nc.tensor.matmul(bk_x[:, E * CAP:2 * E * CAP], xg_lo[:, b, :], rhs,
                                 start=True, stop=True).then_inc(gather_written, 1)

            def quad(m):
                turn(0, m)
                for q in range(4):
                    gather(0, m, q)

            def projections(r, e, n, ic):
                k = IC * n + ic
                if ic == 0:
                    pe.wait_ge(x_in_ready, 16 * (r + 1))
                par = r % 2
                for bk, written, free, base in ((bk_g, gate_written, silu_ready, 0), (bk_u, up_written, hid_f_ready, UP)):
                    if some(k - 1):
                        pe.wait_ge(free, k - 1)
                    at = bass.ds(base + e * I + ic * 128, 128)
                    o = bk[ic % 2][:, :]
                    hi, lo = x_in[:, par, 0, e, :], x_in[:, par, 1, e, :]
                    nc.tensor.matmul(o, ffn_hi[:, at], hi, start=True, stop=False)
                    nc.tensor.matmul(o, ffn_lo[:, at], hi, start=False, stop=False)
                    nc.tensor.matmul(o, ffn_hi[:, at], lo, start=False, stop=True).then_inc(written, 1)

            def down(n, e, par):
                pe.wait_ge(hid_lo_ready, IC * (n + 1))
                if some(n):
                    pe.wait_ge(y_f_ready, n)
                for m in range(M):
                    for ic in range(IC):
                        at = bass.ds(DOWN + e * I + ic * D, D)
                        o = bk_y[:, m * D:(m + 1) * D]
                        hh, hl = (hid[i][par][:, ic, m * 128:(m + 1) * 128] for i in range(2))
                        nc.tensor.matmul(o, hh, ffn_hi[:, at], start=ic == 0, stop=False)
                        nc.tensor.matmul(o, hl, ffn_hi[:, at], start=False, stop=False)
                        t = nc.tensor.matmul(o, hh, ffn_lo[:, at], start=False, stop=ic == IC - 1)
                t.then_inc(down_written, 1)

            def scatter(r, m, bk):
                if m == 0:
                    pe.wait_ge(y_moved, 64 * E * (r + 1))
                a = M * r + m
                pe.wait_ge(back_ready, a + 1)
                if some(a):
                    pe.wait_ge(out_ready, a)
                G = E // 4
                for q in range(4):
                    for g in range(G):
                        for i in range(2):
                            t = nc.tensor.matmul(bk[:, q * D:(q + 1) * D], back[:, m, G * q + g, :],
                                                 y_all[:, g, q, i, m, :], start=g + i == 0,
                                                 stop=(g == G - 1 and i == 1))
                t.then_inc(scatter_written, 1)

            def step(r, e, odd, with_gather, with_scatter):
                n = E * r + e
                m = quad_of(e, odd)
                projections(r, e, n, 0)
                if with_gather and odd:
                    gather(r + 1, m, 1)
                projections(r, e, n, 1)
                if with_scatter:
                    scatter(r - 1, 0, bk_c)
                if with_gather:
                    gather(r + 1, m, 2) if odd else turn(r + 1, m)
                projections(r, e, n, 2)
                if with_scatter:
                    scatter(r - 1, 1, bk_c)
                if not (isinstance(n, int) and n == 0):
                    down(n - 1, e - 1 if not isinstance(e, int) or e > 0 else E - 1, 1 - odd)
                if with_scatter:
                    scatter(r - 1, 2, bk_c)
                if with_gather:
                    gather(r + 1, m, 3 if odd else 0)
                projections(r, e, n, 3)
                if with_scatter:
                    scatter(r - 1, 3, bk_c)

            each_quad(pe, quad)
            rounds(pe, step)
            down(E * R - 1, E - 1, 1)
            pe.wait_ge(x_in_ready, 16 * R)
            for m in range(M):
                scatter(R - 1, m, (bk_c, bk_x)[m % 2])

        @block.scalar
        def _(act):
            def x_in_part(r1, m, q):
                a = 4 * (4 * r1 + m) + q
                act.wait_ge(gather_written, a + 1)
                if some(IC * E * (r1 - 1)):
                    act.wait_ge(up_written, IC * E * (r1 - 1))
                for i in range(2):
                    c = nc.scalar.copy(x_in[:, r1 % 2, i, :, bass.ds(m * 128 + q * CAP, CAP)],
                                       bk_x[:, i * E * CAP:(i + 1) * E * CAP].rearrange("p (a b) -> p a b", a=E))
                c.then_inc(x_in_ready, 1)

            def quad(m):
                for q in range(4):
                    x_in_part(0, m, q)

            def gate(n, ic):
                k = IC * n + ic
                act.wait_ge(gate_written, k + 1)
                if some(k - 1):
                    act.wait_ge(hid_f_ready, k - 1)
                nc.scalar.activation(silu[ic % 2][:, :], bk_g[ic % 2][:, :], ACT.Silu,
                                     scale=1.0 / WSCALE).then_inc(silu_ready, 1)

            def hid_hi(n, ic, par):
                k = IC * n + ic
                act.wait_ge(hid_f_ready, k + 1)
                nc.scalar.copy(hid[0][par][:, ic, :], hid_f[ic % 2][:, :]).then_inc(hid_hi_ready, 1)

            def y_hi(n):
                act.wait_ge(y_f_ready, n + 1)
                if some(n):
                    act.wait_ge(y_moved, 64 * n)
                nc.scalar.copy(y[:, 0, :, :].rearrange("p a b -> p (a b)"), y_f[:, :]).then_inc(y_hi_ready, 1)

            def step(r, e, odd, with_gather, with_scatter):
                n = E * r + e
                m = quad_of(e, odd)
                first = isinstance(n, int) and n == 0
                if not first:
                    hid_hi(n - 1, IC - 1, 1 - odd)
                gate(n, 0)
                if with_gather and odd:
                    x_in_part(r + 1, m, 1)
                gate(n, 1)
                hid_hi(n, 0, odd)
                if with_gather and odd:
                    x_in_part(r + 1, m, 2)
                gate(n, 2)
                hid_hi(n, 1, odd)
                hid_hi(n, 2, odd)
                gate(n, 3)
                if with_gather:
                    x_in_part(r + 1, m, 3 if odd else 0)
                if not first:
                    y_hi(n - 1)

            each_quad(act, quad)
            rounds(act, step)
            hid_hi(E * R - 1, IC - 1, 1)
            y_hi(E * R - 1)

        @block.gpsimd
        def _(pool):
            def hid_lo(n, ic, par):
                k = IC * n + ic
                pool.wait_ge(hid_hi_ready, k + 1)
                nc.gpsimd.tensor_tensor(hid[1][par][:, ic, :], hid_f[ic % 2][:, :], hid[0][par][:, ic, :],
                                        ALU.subtract).then_inc(hid_lo_ready, 1)

            def y_lo(n):
                pool.wait_ge(y_hi_ready, n + 1)
                part = [y[:, i, :, :].rearrange("p a b -> p (a b)") for i in range(2)]
                nc.gpsimd.tensor_tensor(part[1], y_f[:, :], part[0], ALU.subtract).then_inc(y_lo_ready, 1)

            def step(r, e, odd, with_gather, with_scatter):
                n = E * r + e
                first = isinstance(n, int) and n == 0
                if not first:
                    hid_lo(n - 1, IC - 1, 1 - odd)
                for ic in range(IC - 1):
                    hid_lo(n, ic, odd)
                if not first:
                    y_lo(n - 1)

            rounds(pool, step)
            hid_lo(E * R - 1, IC - 1, 1)
            y_lo(E * R - 1)

        @block.vector
        def _(dve):
            iota_e = iota[:, :].rearrange("p (a b) -> p a b", a=1).to_broadcast([128, E, S])

            def one_hot(dst, quad):
                return nc.vector.tensor_tensor(
                    dst, iota_e,
                    pick[:, quad, :, :].rearrange("p a (b c) -> p (a b) c", c=1).to_broadcast([128, E, S]), ALU.is_equal)

            def hot_rows(r1, m):
                a = 4 * r1 + m
                if some(a):
                    dve.wait_ge(hot_written, a)
                one_hot(hot_t[:, :, :], a).then_inc(hot_t_ready, 1)

            def hot_columns(r1, m):
                a = 4 * r1 + m
                dve.wait_ge(hot_written, a + 1)
                if some(4 * a):
                    dve.wait_ge(gather_written, 4 * a)
                nc.vector.tensor_copy(hot[:, :, :].rearrange("p a b -> p (a b)"),
                                      bk_h[:, :]).then_inc(hot_ready, 1)

            def quad(m):
                hot_rows(0, m)
                hot_columns(0, m)

            def hidden(n, ic):
                k = IC * n + ic
                dve.wait_ge(silu_ready, k + 1)
                dve.wait_ge(up_written, k + 1)
                if some(k - 1):
                    dve.wait_ge(hid_lo_ready, k - 1)
                nc.vector.tensor_tensor(hid_f[ic % 2][:, :], bk_u[ic % 2][:, :], silu[ic % 2][:, :],
                                        ALU.mult).then_inc(hid_f_ready, 1)

            def gated(n, r, e):
                dve.wait_ge(down_written, n + 1)
                if some(n):
                    dve.wait_ge(y_lo_ready, n)
                nc.vector.tensor_tensor(
                    y_f[:, :].rearrange("p (a b) -> p a b", a=M), bk_y[:, :].rearrange("p (a b) -> p a b", a=M),
                    gain[:, bass.ds(M * r, M), e].rearrange("p (a b) -> p a b", b=1).to_broadcast([128, M, D]),
                    ALU.mult).then_inc(y_f_ready, 1)

            def add(r, m, bk):
                a = M * r + m
                dve.wait_ge(scatter_written, a + 1)
                at = x_sb[:, bass.ds(16 * r + 4 * m, 4), :]
                nc.vector.scalar_tensor_tensor(
                    out=at, in0=bk[:, :].rearrange("p (a b) -> p a b", a=4), scalar=1.0 / WSCALE,
                    in1=at, op0=ALU.mult, op1=ALU.add).then_inc(out_ready, 1)

            def step(r, e, odd, with_gather, with_scatter):
                n = E * r + e
                m = quad_of(e, odd)
                if with_gather and not odd:
                    hot_rows(r + 1, m)
                hidden(n, 0)
                hidden(n, 1)
                if with_gather and not odd:
                    hot_columns(r + 1, m)
                if with_scatter:
                    add(r - 1, 0, bk_c)
                hidden(n, 2)
                if with_scatter:
                    add(r - 1, 1, bk_c)
                if odd:
                    if some(M * (r - 1)):
                        dve.wait_ge(scatter_written, M * (r - 1) + m + 1)
                    one_hot(back[:, m, :, :], M * r + m).then_inc(back_ready, 1)
                if not (isinstance(n, int) and n == 0):
                    if isinstance(e, int) and e == 0:
                        gated(n - 1, r - 1, E - 1)
                    else:
                        gated(n - 1, r, e - 1)
                if with_scatter:
                    add(r - 1, 2, bk_c)
                hidden(n, 3)
                if with_scatter:
                    add(r - 1, 3, bk_c)

            each_quad(dve, quad)
            rounds(dve, step)
            gated(E * R - 1, R - 1, E - 1)
            for m in range(M):
                add(R - 1, m, (bk_c, bk_x)[m % 2])


def kernel(x, ctx_1024, fside_1x1xSxS2_0, L0_xattn_Wq, L0_xattn_Wk, L0_xattn_Wv, L0_xattn_Wp,
           L0_ffn_gate_w, L0_ffn_w_gate, L0_ffn_w_up, L0_ffn_w_down):
    import numpy as np
    import concourse.bacc as bacc
    from concourse.bass_utils import run_bass_kernel_spmd

    x, context, bias = (np.asarray(a) for a in (x, ctx_1024, fside_1x1xSxS2_0))
    wq, wk, wv, wp = (np.asarray(a) for a in (L0_xattn_Wq, L0_xattn_Wk, L0_xattn_Wv, L0_xattn_Wp))
    gate_w, w_gate, w_up, w_down = (np.asarray(a) for a in (
        L0_ffn_gate_w, L0_ffn_w_gate, L0_ffn_w_up, L0_ffn_w_down))
    d, e, i = x.shape[2], w_gate.shape[0], w_gate.shape[1]
    arrays = {
        "x": x.transpose(1, 0, 2),
        "ctx_t": context.transpose(2, 0, 1),
        "bias": bias[0, 0],
        "wqkv_t": np.concatenate([wq.T, wk.T, wv.T], axis=1),
        "wp_t": wp.T.reshape(-1, 128, d).transpose(1, 0, 2),
        "gate_t": gate_w.T,
        "ffn_w": np.concatenate([
            w_gate.transpose(2, 0, 1).reshape(d, e * i),
            w_up.transpose(2, 0, 1).reshape(d, e * i),
            w_down.transpose(2, 0, 1).reshape(i // 128, 128, e, d).transpose(1, 2, 0, 3).reshape(128, e * i),
        ], axis=1),
    }
    arrays = {name: np.ascontiguousarray(a) for name, a in arrays.items()}
    nc = bacc.Bacc("TRN2", target_bir_lowering=False, num_devices=1)
    args = [nc.dram_tensor(name, a.shape, mybir.dt.from_np(a.dtype), kind="ExternalInput").ap()
            for name, a in arrays.items()]
    out = nc.dram_tensor("out", arrays["x"].shape, F32, kind="ExternalOutput").ap()
    cross_attention_moe_kernel(nc, *args, out)
    got = run_bass_kernel_spmd(nc, [arrays], core_ids=[0])
    return np.ascontiguousarray(got.results[0]["out"].transpose(1, 0, 2))
```

```python
from contextlib import ExitStack

import concourse.bass as bass
from concourse import mybir

ALU = mybir.AluOpType
ACT = mybir.ActivationFunctionType
AX = mybir.AxisListType.X
F32 = mybir.dt.float32
F16 = mybir.dt.float16
U32 = mybir.dt.uint32

EPS = 1e-5
WSCALE = 16.0
FRONT = 5
DRAIN = 3


def cross_attention_moe_kernel(nc, x, ctx_t, bias, wqkv_t, wp_t, gate_t, ffn_w, out):
    S, B, D = x.shape
    K = ctx_t.shape[2]
    HD = wqkv_t.shape[1] // 3
    PAIRS = wp_t.shape[1]
    H = 2 * PAIRS
    DH = HD // H
    GROUPS = 4
    GH = H // GROUPS
    GP = PAIRS // GROUPS
    E = gate_t.shape[1]
    I = ffn_w.shape[1] // (3 * E)
    CAP = S // E * 2
    WCH = ffn_w.shape[1] // B
    SCORE = float(D) ** -0.5 / (WSCALE * WSCALE)
    assert S == 128 and D == 128 and DH == 64 and B % 16 == 0 and CAP == 32

    QK = GP * (S + K)
    OW = DH + 1

    with ExitStack() as ctx:
        def sb(name, shape, dt):
            return ctx.enter_context(nc.sbuf_tensor(name, shape, dt))

        def sem(name):
            return ctx.enter_context(nc.semaphore(name))

        x_sb = sb("x_sb", [S, B, D], F32)
        xg_hi = sb("xg_hi", [S, B, D], F16)
        xg_lo = sb("xg_lo", [S, B, D], F16)
        ffn_hi = sb("ffn_hi", [D, 3 * E * I], F16)
        ffn_lo = sb("ffn_lo", [D, 3 * E * I], F16)
        logits = sb("logits", [S, B, E], F32)
        ident = sb("ident", [128, 128], F32)
        ident_h = sb("ident_h", [128, 128], F16)
        iota = sb("iota", [128, 128], F32)
        gate_sb = sb("gate_sb", [D, E], F32)

        pick = sb("pick", [128, B // 4, 4, E // 4], F32)
        gain = sb("gain", [128, B // 4, E], F32)

        attention(nc, locals())
        experts(nc, locals())


def attention(nc, v):
    x, ctx_t, bias, wqkv_t, wp_t, gate_t, ffn_w = (v[n] for n in (
        "x", "ctx_t", "bias", "wqkv_t", "wp_t", "gate_t", "ffn_w"))
    S, B, D, K, HD, H, DH, E = (v[n] for n in ("S", "B", "D", "K", "HD", "H", "DH", "E"))
    PAIRS, GROUPS, GH, GP, WCH, SCORE, QK, OW = (v[n] for n in (
        "PAIRS", "GROUPS", "GH", "GP", "WCH", "SCORE", "QK", "OW"))
    x_sb, xg_hi, xg_lo, ffn_hi, ffn_lo, logits, ident, ident_h, iota, gate_sb = (v[n] for n in (
        "x_sb", "xg_hi", "xg_lo", "ffn_hi", "ffn_lo", "logits", "ident", "ident_h", "iota", "gate_sb"))

    with ExitStack() as ctx:
        def sb(name, shape, dt):
            return ctx.enter_context(nc.sbuf_tensor(name, shape, dt))

        def two(name, shape, dt):
            return [sb(f"{name}{i}", shape, dt) for i in range(2)]

        def bank(name):
            return ctx.enter_context(nc.psum_tensor(name, [128, 512], F32))

        sem = v["sem"]

        w_hi = sb("w_hi", [D, 3 * HD], F16)
        w_lo = sb("w_lo", [D, 3 * HD], F16)
        wp_sb = sb("wp_sb", [2 * DH, PAIRS, D], F32)
        bias_sb = sb("bias_sb", [S, K], F32)
        half = sb("half", [128, 2], F32)
        ctx_f = two("ctx_f", [D, K], F32)
        ctx_hi = two("ctx_hi", [D, K], F16)
        ctx_lo = two("ctx_lo", [D, K], F16)
        wst = two("wst", [D, WCH], F32)
        wsc = sb("wsc", [D, WCH], F32)
        stats = sb("stats", [S, 2, 6], F32)
        mv = sb("mv", [S, 2, 2], F32)
        vpe = sb("vpe", [S, 2], F32)
        rstd = sb("rstd", [S, 2], F32)
        xn = sb("xn", [S, D], F32)
        xn_hi = sb("xn_hi", [S, D], F16)
        xn_lo = sb("xn_lo", [S, D], F16)
        xn2 = sb("xn2", [S, D], F32)
        xT = two("xT", [D, 2, S], F16)
        x2T = sb("x2T", [D, S], F32)
        qk_hi = two("qk_hi", [128, GROUPS, QK], F16)
        qk_lo = two("qk_lo", [128, GROUPS, QK], F16)
        v_hi = two("v_hi", [128, H, OW], F16)
        v_lo = two("v_lo", [128, H, DH], F16)
        v_f = two("v_f", [128, GH, DH], F32)
        neg = two("neg", [S, GH, K], F32)
        negmax = two("negmax", [S, GH], F32)
        probs = two("probs", [S, GH, K], F32)
        pT_hi = two("pT_hi", [128, GH, S], F16)
        pT_lo = two("pT_lo", [128, GH, S], F16)
        rsum = sb("rsum", [S, GH], F32)
        o_sb = two("o_sb", [S, GH, DH], F32)
        oT = two("oT", [2 * DH, GP, S], F32)
        w_f = sb("w_f", [D, 3 * HD], F32)

        bk_s = [bank("bk_s0"), bank("bk_s1")]
        bk_t, bk_a, bk_b, bk_o, bk_x, bk_y = (bank(n) for n in (
            "bk_t", "bk_a", "bk_b", "bk_o", "bk_x", "bk_y"))

        loaded_wv, loaded_wq, loaded_wk = sem("loaded_wv"), sem("loaded_wq"), sem("loaded_wk")
        loaded_b, loaded = sem("loaded_b"), sem("loaded")
        weight_parts = ((loaded_wv, slice(2 * HD, 3 * HD)), (loaded_wq, slice(0, HD)), (loaded_wk, slice(HD, 2 * HD)))
        const_ready = sem("const_ready")
        ident_h_ready = sem("ident_h_ready")
        w_hi_ready, w_ready = sem("w_hi_ready"), sem("w_ready")
        bias_ready = sem("bias_ready")
        ctx_ready, ffnw_ready = sem("ctx_ready"), sem("ffnw_ready")
        pool_chain, dve_chain = sem("pool_chain"), sem("dve_chain")
        stats_ready, rstd_ready = sem("stats_ready"), sem("rstd_ready")
        xn_ready, xn2_ready = sem("xn_ready"), sem("xn2_ready")
        xg_ready = sem("xg_ready")
        xT_written, x2T_written = sem("xT_written"), sem("x2T_written")
        xn_parts_ready, xT_ready, x2T_ready = sem("xn_parts_ready"), sem("xT_ready"), sem("x2T_ready")
        qk_written, qk_hi_ready, qk_lo_ready = sem("qk_written"), sem("qk_hi_ready"), sem("qk_lo_ready")
        v_written, v_hi_ready, v_lo_ready = sem("v_written"), sem("v_hi_ready"), sem("v_lo_ready")
        scores_written, neg_ready, probs_ready = sem("scores_written"), sem("neg_ready"), sem("probs_ready")
        pT_written, pT_hi_ready, pT_lo_ready = sem("pT_written"), sem("pT_hi_ready"), sem("pT_lo_ready")
        pv_written, o_ready = sem("pv_written"), sem("o_ready")
        oT_written, oT_ready = sem("oT_written"), sem("oT_ready")
        proj_written, x1_ready = sem("proj_written"), sem("x1_ready")
        logits_written, logits_ready = sem("logits_written"), sem("logits_ready")

        first, last = -1, B + DRAIN
        loop_end = B - 1
        assert (loop_end - FRONT) % 2 == 0

        def live(b):
            return not isinstance(b, int) or 0 <= b < B

        def upto(count):
            return min(count, B) if isinstance(count, int) else count

        def some(count):
            return not isinstance(count, int) or count > 0

        def alone(eng):
            eng.nop(nofuse=True)

        def slots(eng, slot, end=last, loop_end=loop_end, first=first):
            for t in range(first, FRONT):
                slot(t, t % 2)
            with eng.Fori(FRONT, loop_end - 1, 2) as t:
                slot(t, FRONT % 2)
                slot(t + 1, (FRONT + 1) % 2)
            for t in range(loop_end, end):
                slot(t, t % 2)

        def behind(t, g, k):
            return t - 1 + (g - k) // GROUPS, (g - k) % GROUPS

        block = ctx.enter_context(nc.Block())

        @block.sync
        def _(sp):
            def slot(t, par):
                if some(t * 48):
                    sp.wait_ge(loaded, t * 48)
                sp.dma_start(x_sb[:, t, :], x[:, t, :]).then_inc(loaded, 16)
                if some(t - 1):
                    sp.wait_ge(ctx_ready, t - 1)
                sp.dma_start(ctx_f[par][:, :], ctx_t[:, t, :]).then_inc(loaded, 16)
                if some(t - 1):
                    sp.wait_ge(ffnw_ready, t - 1)
                src = ffn_w[:, bass.ds(t * WCH, WCH)] if not isinstance(t, int) else ffn_w[:, t * WCH:(t + 1) * WCH]
                sp.dma_start(wst[par][:, :], src).then_inc(loaded, 16)

            slots(sp, slot, end=B, first=0)

        @block.gpsimd
        def _(pool):
            pool.memset(ident[:, :], 0.0).then_inc(pool_chain, 1)
            pool.memset(half[:, :], -0.5).then_inc(const_ready, 1)
            pool.memset(vpe[:, :], 1.0).then_inc(const_ready, 1)
            pool.memset(mv[:, :, :], 1.0).then_inc(const_ready, 1)
            for i in range(2):
                pool.memset(v_hi[i][:, :, DH:OW], 1.0).then_inc(const_ready, 1)
            pool.wait_ge(pool_chain, 1)
            pool.affine_select(out=ident[:, :], in_=ident[:, :], compare_op=ALU.not_equal, fill=1.0,
                               base=0, pattern=[[-1, 128]], channel_multiplier=1).then_inc(const_ready, 1)
            pool.iota(iota[:, :], pattern=[[1, 128]], base=0, channel_multiplier=0,
                      allow_small_or_imprecise_dtypes=True).then_inc(const_ready, 1)
            pool.wait_ge(const_ready, 7)
            pool.tensor_copy(ident_h[:, :], ident[:, :]).then_inc(ident_h_ready, 1)

            def values(t, g, par):
                if live(t):
                    pool.wait_ge(v_hi_ready, 4 * t + g + 1)
                    if some(4 * (t - 2) + g + 1):
                        pool.wait_ge(pv_written, 4 * (t - 2) + g + 1)
                    pool.tensor_tensor(v_lo[par][0:K, GH * g:GH * (g + 1), :], v_f[g % 2][0:K, :, :],
                                       v_hi[par][0:K, GH * g:GH * (g + 1), 0:DH], ALU.subtract).then_inc(v_lo_ready, 1)

            def slot(t, par):
                c = chain(t)
                at = slice(t * WCH, (t + 1) * WCH) if isinstance(t, int) else bass.ds(t * WCH, WCH)
                i = (par + 1) % 2
                values(t - 1, GROUPS - 1, i)
                pool.wait_ge(stats_ready, t + 2)
                alone(pool)
                pool.tensor_scalar(vpe[:, :], mv[:, :, 1], EPS, None, ALU.add).then_inc(pool_chain, 1)
                pool.wait_ge(pool_chain, c[0])
                if some(upto(t + 1)):
                    pool.wait_ge(xn_ready, upto(t + 1))
                if some(t - 3):
                    pool.wait_ge(xn2_ready, t - 3)
                pool.tensor_tensor(rstd[:, :], vpe[:, :], half[:, :], ALU.pow).then_inc(rstd_ready, 1)
                if live(t + 1):
                    pool.wait_ge(loaded, (t + 2) * 48)
                    if some(4 * t):
                        pool.wait_ge(v_written, 4 * t)
                    alone(pool)
                    pool.tensor_copy(ctx_hi[i][:, :], ctx_f[i][:, :]).then_inc(pool_chain, 1)
                if live(t):
                    if some(t):
                        pool.wait_ge(ffnw_ready, t)
                    alone(pool)
                    pool.tensor_scalar(wsc[:, :], wst[par][:, :], WSCALE, None, ALU.mult).then_inc(pool_chain, 1)
                values(t, 0, par)
                if live(t + 1):
                    pool.wait_ge(pool_chain, c[1])
                    pool.tensor_tensor(ctx_lo[i][:, :], ctx_f[i][:, :], ctx_hi[i][:, :],
                                       ALU.subtract).then_inc(ctx_ready, 1)
                    pool.wait_ge(xn_ready, t + 2)
                    if some(t + 1):
                        pool.wait_ge(xT_written, t + 1)
                    alone(pool)
                    pool.tensor_copy(xn_hi[:, :], xn[:, :]).then_inc(pool_chain, 1)
                    pool.wait_ge(pool_chain, c[3])
                    pool.tensor_tensor(xn_lo[:, :], xn[:, :], xn_hi[:, :], ALU.subtract).then_inc(xn_parts_ready, 1)
                values(t, 1, par)
                if live(t):
                    pool.wait_ge(pool_chain, c[2])
                    alone(pool)
                    pool.tensor_copy(ffn_hi[:, at], wsc[:, :]).then_inc(pool_chain, 1)
                if live(t - 3):
                    pool.wait_ge(xn2_ready, t - 2)
                    alone(pool)
                    pool.tensor_copy(xg_hi[:, t - 3, :], xn2[:, :]).then_inc(pool_chain, 1)
                values(t, 2, par)
                if live(t):
                    pool.wait_ge(pool_chain, c[4])
                    pool.tensor_tensor(ffn_lo[:, at], wsc[:, :], ffn_hi[:, at], ALU.subtract).then_inc(ffnw_ready, 1)
                if live(t - 3):
                    pool.wait_ge(pool_chain, c[5])
                    pool.tensor_tensor(xg_lo[:, t - 3, :], xn2[:, :], xg_hi[:, t - 3, :],
                                       ALU.subtract).then_inc(xg_ready, 1)

            def chain(t):
                def before(lag, each):
                    return each * (t - lag) if not isinstance(t, int) else each * min(max(t - lag, 0), B)
                c = 1 + (t + 1) + before(-1, 2) + before(0, 2) + before(3, 1)
                out = [c + 1]
                for batch in (t + 1, t, t + 1, t, t - 3):
                    out.append(out[-1] + (1 if live(batch) else 0))
                return out

            slots(pool, slot)

        @block.scalar
        def _(act):
            for loaded_part, at in weight_parts:
                act.dma_start(w_f[:, at], wqkv_t[:, at]).then_inc(loaded_part, 16)
            act.dma_start(bias_sb[:, :], bias).then_inc(loaded_b, 16)
            act.dma_start(wp_sb[:, :, :], wp_t).then_inc(loaded_b, 16)
            act.dma_start(gate_sb[:, :], gate_t).then_inc(loaded_b, 16)
            for loaded_part, at in weight_parts:
                act.wait_ge(loaded_part, 16)
                nc.scalar.activation(w_hi[:, at], w_f[:, at], ACT.Copy, scale=WSCALE).then_inc(w_hi_ready, 1)

            def step(t, par, g):
                n = 4 * (t - 1) + g
                tw, gw, pw = (t, g - 1, par) if g else (t - 1, GROUPS - 1, (par + 1) % 2)
                b4, g4 = behind(t, g, 4)
                if live(b4):
                    act.wait_ge(oT_written, 4 * b4 + g4 + 1)
                    if some(4 * b4 + g4 - 1):
                        act.wait_ge(proj_written, 4 * b4 + g4 - 1)
                    nc.scalar.copy(oT[g4 % 2][:, :, :].rearrange("p a b -> p (a b)"),
                                   bk_x[:, 0:GP * S]).then_inc(oT_ready, 1)
                if gw == 2 and live(tw - 3):
                    act.wait_ge(x2T_written, tw - 2)
                    if live(b4):
                        act.wait_ge(oT_written, 4 * b4 + g4 + 1)
                    if some(tw - 3):
                        act.wait_ge(logits_written, tw - 3)
                    nc.scalar.copy(x2T[:, :], bk_x[:, 384:512]).then_inc(x2T_ready, 1)
                if live(tw):
                    act.wait_ge(qk_written, 4 * tw + gw + 1)
                    if some(4 * (tw - 2) + gw + 1):
                        act.wait_ge(scores_written, 4 * (tw - 2) + gw + 1)
                    nc.scalar.copy(qk_hi[pw][:, gw, :], bk_a[:, 0:QK]).then_inc(qk_hi_ready, 1)
                if gw == GROUPS - 1 and live(tw - 3):
                    act.wait_ge(logits_written, tw - 2)
                    if live(tw):
                        act.wait_ge(v_written, 4 * tw + gw + 1)
                    nc.scalar.copy(logits[:, tw - 3, :], bk_b[:, 256:256 + E]).then_inc(logits_ready, 1)
                if live(tw):
                    act.wait_ge(v_written, 4 * tw + gw + 1)
                    if some(4 * tw + gw - 1):
                        act.wait_ge(v_lo_ready, 4 * tw + gw - 1)
                    values = bk_b[0:K, 0:GH * DH].rearrange("p (a b) -> p a b", a=GH)
                    nc.scalar.copy(v_f[gw % 2][0:K, :, :], values)
                    if some(4 * (tw - 2) + gw + 1):
                        act.wait_ge(pv_written, 4 * (tw - 2) + gw + 1)
                    nc.scalar.copy(v_hi[pw][0:K, GH * gw:GH * (gw + 1), 0:DH], values).then_inc(v_hi_ready, 1)
                if gw == 2 and live(tw + 1):
                    act.wait_ge(xT_written, tw + 2)
                    if some(4 * tw):
                        act.wait_ge(qk_written, 4 * tw)
                    nc.scalar.copy(xT[(pw + 1) % 2][:, :, :].rearrange("p a b -> p (a b)"),
                                   bk_x[:, 256:384].bitcast(F16)).then_inc(xT_ready, 1)
                b1, g1 = behind(t, g, 1)
                if live(b1):
                    act.wait_ge(pT_written, 4 * b1 + g1 + 1)
                    if some(4 * b1 + g1 - 1):
                        act.wait_ge(pv_written, 4 * b1 + g1 - 1)
                    nc.scalar.copy(pT_hi[g1 % 2][0:K, :, :].rearrange("p a b -> p (a b)"),
                                   bk_t[0:K, :]).then_inc(pT_hi_ready, 1)
                if live(t - 1):
                    act.wait_ge(neg_ready, n + 1)
                    if some(n - 1):
                        act.wait_ge(pT_written, n - 1)
                    for i in range(GH):
                        e = nc.scalar.activation(probs[g % 2][:, i, :], neg[g % 2][:, i, :], ACT.Exp,
                                                 bias=negmax[g % 2][:, i:i + 1], scale=-1.0)
                    e.then_inc(probs_ready, 1)

            slots(act, lambda t, par: [step(t, par, g) for g in range(GROUPS)])
            step(last, last % 2, 0)

        @block.vector
        def _(dve):
            dve.wait_ge(const_ready, 7)

            def chain(t):
                if not isinstance(t, int):
                    return (t + 1) + (t - 2) + 4 * (t - 1) - 2
                part = lambda lag: min(max(t - lag, 0), B)
                return part(-1) + part(2) + max(min(4 * (t - 1) - 2, 4 * B), 0)

            def step(t, par, g, c):
                n = 4 * (t - 1) + g
                tw, gw, pw = (t, g - 1, par) if g else (t - 1, GROUPS - 1, (par + 1) % 2)
                if live(t - 1):
                    dve.wait_ge(scores_written, n + 1)
                    if some(n - 1):
                        dve.wait_ge(probs_ready, n - 1)
                    alone(dve)
                    for i in range(GH):
                        r = nc.vector.tensor_tensor_reduce(
                            out=neg[g % 2][:, i, :], in0=bk_s[i % 2][:, (i // 2) * K:(i // 2 + 1) * K],
                            in1=bias_sb[:, :], scale=-SCORE, scalar=3.0e38, op0=ALU.add, op1=ALU.min,
                            accum_out=negmax[g % 2][:, i:i + 1])
                    r.then_inc(neg_ready, 1)
                if live(tw):
                    dve.wait_ge(qk_hi_ready, 4 * tw + gw + 1)
                    if some(4 * (tw - 2) + gw + 1):
                        dve.wait_ge(scores_written, 4 * (tw - 2) + gw + 1)
                    nc.vector.tensor_tensor(qk_lo[pw][:, gw, :], bk_a[:, 0:QK], qk_hi[pw][:, gw, :],
                                            ALU.subtract).then_inc(qk_lo_ready, 1)
                if g == 0 and live(t + 1):
                    dve.wait_ge(loaded, (t + 2) * 48)
                    alone(dve)
                    nc.vector.bn_stats(stats[:, 0, :], x_sb[:, t + 1, :]).then_inc(dve_chain, 1)
                    c = c + 1
                stats_count = c
                b2, g2 = behind(t, g, 2)
                if live(b2):
                    dve.wait_ge(pv_written, 4 * b2 + g2 + 1)
                    o = bk_o[:, 0:GH * OW].rearrange("p (a b) -> p a b", a=GH)
                    nc.vector.reciprocal(rsum[:, :], o[:, :, DH]).then_inc(dve_chain, 1)
                    c = c + 1
                if g == 0:
                    if some(stats_count):
                        dve.wait_ge(dve_chain, stats_count)
                    if some(t + 1):
                        dve.wait_ge(rstd_ready, t + 1)
                    alone(dve)
                    for k in [k for k, b in ((0, t + 1), (1, t - 3)) if live(b)]:
                        a = nc.vector.bn_aggr(mv[:, k, :], stats[:, k, :])
                    a.then_inc(stats_ready, 1)
                b1, g1 = behind(t, g, 1)
                if live(b1):
                    dve.wait_ge(pT_hi_ready, 4 * b1 + g1 + 1)
                    if some(4 * b1 + g1 - 1):
                        dve.wait_ge(pv_written, 4 * b1 + g1 - 1)
                    nc.vector.tensor_tensor(pT_lo[g1 % 2][0:K, :, :].rearrange("p a b -> p (a b)"), bk_t[0:K, :],
                                            pT_hi[g1 % 2][0:K, :, :].rearrange("p a b -> p (a b)"),
                                            ALU.subtract).then_inc(pT_lo_ready, 1)
                if live(b2):
                    dve.wait_ge(dve_chain, c)
                    if some(4 * b2 + g2 - 1):
                        dve.wait_ge(oT_written, 4 * b2 + g2 - 1)
                    nc.vector.scalar_tensor_tensor(
                        out=o_sb[g2 % 2][:, :, :], in0=o[:, :, 0:DH], scalar=1.0 / WSCALE,
                        in1=rsum[:, :].rearrange("p (a b) -> p a b", b=1).to_broadcast([S, GH, DH]),
                        op0=ALU.mult, op1=ALU.mult).then_inc(o_ready, 1)
                if g == 1:
                    dve.wait_ge(rstd_ready, t + 2)
                    if live(t + 1):
                        if some(t + 1):
                            dve.wait_ge(xn_parts_ready, t + 1)
                        nc.vector.tensor_scalar(xn[:, :], x_sb[:, t + 1, :], mv[:, 0, 0:1], rstd[:, 0:1],
                                                ALU.subtract, ALU.mult).then_inc(xn_ready, 1)
                    if live(t - 3):
                        if some(t - 3):
                            dve.wait_ge(x2T_written, t - 3)
                        if some(t - 3):
                            dve.wait_ge(xg_ready, t - 3)
                        nc.vector.tensor_scalar(xn2[:, :], x_sb[:, t - 3, :], mv[:, 1, 0:1], rstd[:, 1:2],
                                                ALU.subtract, ALU.mult).then_inc(xn2_ready, 1)
                if g == GROUPS - 1 and live(t - 2):
                    dve.wait_ge(proj_written, 4 * (t - 2) + 4)
                    nc.vector.tensor_tensor(x_sb[:, t - 2, :], x_sb[:, t - 2, :], bk_y[:, 0:D],
                                            ALU.add).then_inc(x1_ready, 1)
                    dve.wait_ge(x1_ready, t - 1)
                    alone(dve)
                    nc.vector.bn_stats(stats[:, 1, :], x_sb[:, t - 2, :]).then_inc(dve_chain, 1)
                    c = c + 1
                return c

            def slot(t, par):
                c = chain(t)
                for g in range(GROUPS):
                    c = step(t, par, g, c)

            slot(first, first % 2)
            for i in range(3):
                at = weight_parts[i][1]
                dve.wait_ge(w_hi_ready, i + 1)
                nc.vector.scalar_tensor_tensor(out=w_lo[:, at], in0=w_f[:, at], scalar=WSCALE, in1=w_hi[:, at],
                                               op0=ALU.mult, op1=ALU.subtract).then_inc(w_ready, 1)
            dve.wait_ge(loaded_b, 48)
            nc.vector.tensor_scalar(bias_sb[:, :], bias_sb[:, :], 1.0 / SCORE, None,
                                    ALU.mult).then_inc(bias_ready, 1)
            dve.wait_ge(bias_ready, 1)
            slots(dve, slot, first=first + 1)

        @block.tensor
        def _(pe):
            pe.wait_ge(const_ready, 7)
            pe.wait_ge(ident_h_ready, 1)

            def product(out, lhs, rhs, **kw):
                (lh, ll), (rh, rl) = lhs, rhs
                nc.tensor.matmul(out, lh, rh, start=True, stop=False)
                nc.tensor.matmul(out, ll, rh, start=False, stop=False)
                return nc.tensor.matmul(out, lh, rl, start=False, stop=True)

            def step(t, par, g):
                n = 4 * (t - 1) + g
                if live(t - 1):
                    p1 = (par + 1) % 2
                    pe.wait_ge(qk_lo_ready, n + 1)
                    if some(n):
                        pe.wait_ge(neg_ready, n)
                    for j in range(GP):
                        for lo_q, lo_k in ((0, 0), (1, 0), (0, 1)):
                            for h in range(2):
                                r = slice(DH * h, DH * (h + 1))
                                q = (qk_hi, qk_lo)[lo_q][p1][r, g, j * S:(j + 1) * S]
                                k = (qk_hi, qk_lo)[lo_k][p1][r, g, GP * S + j * K:GP * S + (j + 1) * K]
                                m = nc.tensor.matmul(bk_s[h][:, j * K:(j + 1) * K], q, k,
                                                     start=lo_q + lo_k == 0, stop=lo_k == 1)
                    m.then_inc(scores_written, 1)
                b1, g1 = behind(t, g, 1)
                if live(b1):
                    pe.wait_ge(probs_ready, 4 * b1 + g1 + 1)
                    if some(4 * b1 + g1):
                        pe.wait_ge(pT_lo_ready, 4 * b1 + g1)
                    for i in range(GH):
                        m = nc.tensor.transpose(bk_t[0:K, i * S:(i + 1) * S], probs[g1 % 2][:, i, :], ident[:, :])
                    m.then_inc(pT_written, 1)
                b2, g2 = behind(t, g, 2)
                if live(b2):
                    p2 = (par + 1) % 2 if g >= 2 else par
                    pe.wait_ge(pT_lo_ready, 4 * b2 + g2 + 1)
                    pe.wait_ge(v_lo_ready, 4 * b2 + g2 + 1)
                    if some(4 * b2 + g2):
                        pe.wait_ge(o_ready, 4 * b2 + g2)
                    for i in range(GH):
                        h = GH * g2 + i
                        ph, pl = pT_hi[g2 % 2][0:K, i, :], pT_lo[g2 % 2][0:K, i, :]
                        nc.tensor.matmul(bk_o[:, i * OW:(i + 1) * OW], ph, v_hi[p2][0:K, h, :], start=True, stop=False)
                        nc.tensor.matmul(bk_o[:, i * OW:i * OW + DH], ph, v_lo[p2][0:K, h, :], start=False, stop=False)
                        m = nc.tensor.matmul(bk_o[:, i * OW:(i + 1) * OW], pl, v_hi[p2][0:K, h, :], start=False, stop=True)
                    m.then_inc(pv_written, 1)
                if g == 0:
                    if some(upto(t - 3)):
                        pe.wait_ge(logits_ready, upto(t - 3))
                if live(t):
                    if some(4 * t + g):
                        pe.wait_ge(v_hi_ready, 4 * t + g)
                if g == GROUPS - 1 and live(t - 3):
                    pe.wait_ge(x2T_ready, t - 2)
                    nc.tensor.matmul(bk_b[:, 256:256 + E], x2T[:, :], gate_sb[:, :],
                                     start=True, stop=True).then_inc(logits_written, 1)
                if live(t):
                    if g == 0:
                        if isinstance(t, int) and t == 0:
                            pe.wait_ge(w_ready, 1)
                        pe.wait_ge(ctx_ready, t + 1)
                    cT = ctx_hi[par][:, :], ctx_lo[par][:, :]
                    c = 2 * HD + GH * DH * g
                    product(bk_b[0:K, 0:GH * DH], cT, (w_hi[:, c:c + GH * DH], w_lo[:, c:c + GH * DH])
                            ).then_inc(v_written, 1)
                b3, g3 = behind(t, g, 3)
                if live(b3) or g == 2:
                    if live(b3) and some(4 * b3 + g3):
                        pe.wait_ge(oT_ready, 4 * b3 + g3)
                    if g == 3:
                        if live(t + 1) and some(t + 2):
                            pe.wait_ge(xT_ready, t + 2)
                        if live(t - 3) and some(t - 2):
                            pe.wait_ge(x2T_ready, t - 2)
                    if g == 2:
                        if live(t) and some(t + 1):
                            pe.wait_ge(xT_ready, t + 1)
                        if live(t - 3) and some(t - 3):
                            pe.wait_ge(x2T_ready, t - 3)
                        if live(t + 1):
                            pe.wait_ge(xn_parts_ready, t + 2)
                            parts = bk_x[:, 256:384].bitcast(F16)
                            nc.tensor.transpose(parts[:, 0:S], xn_hi[:, :], ident_h[:, :])
                            nc.tensor.transpose(parts[:, S:2 * S], xn_lo[:, :], ident_h[:, :]).then_inc(xT_written, 1)
                        if live(t - 3):
                            pe.wait_ge(xn2_ready, t - 2)
                            nc.tensor.transpose(bk_x[:, 384:512], xn2[:, :], ident[:, :]).then_inc(x2T_written, 1)
                if live(b3):
                    pe.wait_ge(o_ready, 4 * b3 + g3 + 1)
                    for j in range(GP):
                        m = nc.tensor.transpose(bk_x[:, j * S:(j + 1) * S],
                                                o_sb[g3 % 2][:, 2 * j:2 * j + 2, :].rearrange("p a b -> p (a b)"),
                                                ident[:, :])
                    m.then_inc(oT_written, 1)
                b4, g4 = behind(t, g, 4)
                if live(b4):
                    if isinstance(b4, int) and b4 + g4 == 0:
                        pe.wait_ge(loaded_b, 48)
                    pe.wait_ge(oT_ready, 4 * b4 + g4 + 1)
                    if g4 == 0:
                        if some(b4):
                            pe.wait_ge(x1_ready, b4)
                    for j in range(GP):
                        m = nc.tensor.matmul(bk_y[:, 0:D], oT[g4 % 2][:, j, :], wp_sb[:, GP * g4 + j, :],
                                             start=(g4 == 0 and j == 0), stop=(g4 == GROUPS - 1 and j == GP - 1))
                    m.then_inc(proj_written, 1)

                if live(t):
                    if g == 0:
                        if isinstance(t, int) and t == 0:
                            pe.wait_ge(w_ready, 3)
                        pe.wait_ge(xT_ready, t + 1)
                    if some(4 * t + g):
                        pe.wait_ge(qk_lo_ready, 4 * t + g)
                    xp = xT[par][:, 0, :], xT[par][:, 1, :]
                    for j in range(GP):
                        for base, at, wide, r in ((0, j * S, S, xp), (HD, GP * S + j * K, K, cT)):
                            c = base + 2 * DH * (GP * g + j)
                            w = w_hi[:, c:c + 2 * DH], w_lo[:, c:c + 2 * DH]
                            m = product(bk_a[:, at:at + wide], w, r)
                    m.then_inc(qk_written, 1)

            slots(pe, lambda t, par: [step(t, par, g) for g in range(GROUPS)])


def routing(nc, v, scratch, bk_aff, bk_idx):
    S, B, E, CAP = (v[n] for n in ("S", "B", "E", "CAP"))
    logits, ident, pick, gain, sem = (v[n] for n in ("logits", "ident", "pick", "gain", "sem"))
    R = B // 16
    used = [0]

    def part(*shape):
        size = 1
        for n in shape:
            size *= n
        used[0] += size
        names = "abcd"[:len(shape)]
        dims = dict(zip(names, shape))
        flat = scratch[:, used[0] - size:used[0]]
        if len(shape) == 1:
            return flat
        return flat.rearrange(f"p ({' '.join(names)}) -> p {' '.join(names)}", **dims)

    top, total, share = part(B), part(B), part(B)
    shifted, weights = part(B, E), part(B, E)
    aff = part(R, 4, 4, E)
    affT = part(R, S)
    vals, idx_f, idx_g, vals_T = (part(R, CAP) for _ in range(4))
    idx = part(R, CAP).bitcast(U32)
    regroup = part(4, 4, 4, E // 4)
    exp_ready, aff_ready, aff_written, chain = (sem(n) for n in (
        "exp_ready", "aff_ready", "aff_written", "routing_chain"))
    shifted_ready, regroup_ready = sem("shifted_ready"), sem("regroup_ready")
    idx_ready, idx_written = sem("idx_ready"), sem("idx_written")
    count = [0]
    flat = lambda a: a.rearrange("p a b -> p (a b)")

    def done(dve, instruction):
        count[0] += 1
        instruction.then_inc(chain, 1)
        dve.wait_ge(chain, count[0])

    def take(dve, k, first, end):
        at, back = slice(8 * k, 8 * (k + 1)), end - first - 1
        for r in range(first, end):
            if k:
                dve.wait_ge(chain, count[0] - back)
            nc.vector.max(vals[:, r, at], affT[:, r, :]).then_inc(chain, 1)
            count[0] += 1
        for r in range(first, end):
            dve.wait_ge(chain, count[0] - back)
            nc.vector.max_index(idx[:, r, at], vals[:, r, at], affT[:, r, :]).then_inc(chain, 1)
            count[0] += 1
        for r in range(first, end):
            dve.wait_ge(chain, count[0] - back)
            nc.vector.match_replace(out=affT[:, r, :], in_to_replace=vals[:, r, at],
                                    in_values=affT[:, r, :], imm_value=-1.0).then_inc(chain, 1)
            count[0] += 1

    def regrouped(pe, call, first, end):
        pe.wait_ge(idx_ready, call)
        nc.tensor.matmul(bk_idx[:, CAP * first:CAP * end], regroup.rearrange("p a b c d -> p (a b c d)"),
                         flat(idx_f[:, first:end, :]), start=True, stop=True).then_inc(idx_written, 1)

    def tokens(dve, call, first, end):
        quads = slice(4 * first, 4 * end)
        dve.wait_ge(chain, count[0])
        nc.vector.tensor_copy(idx_f[:, first:end, :], idx[:, first:end, :]).then_inc(idx_ready, 1)
        done(dve, nc.vector.transpose(flat(vals_T[:, first:end, :]), flat(vals[:, first:end, :])))
        done(dve, nc.vector.tensor_scalar(flat(gain[:, quads, :]), flat(vals_T[:, first:end, :]), 1.0 / WSCALE,
                                          None, ALU.mult))
        dve.wait_ge(idx_written, call)
        done(dve, nc.vector.tensor_copy(flat(idx_g[:, first:end, :]), bk_idx[:, CAP * first:CAP * end]))
        done(dve, nc.vector.transpose(pick[:, quads, :, :].rearrange("p a b c -> p (a b c)"),
                                      flat(idx_g[:, first:end, :])))

    with nc.Block() as block:
        @block.scalar
        def _(act):
            act.wait_ge(shifted_ready, 1)
            nc.scalar.activation(weights, shifted, ACT.Exp).then_inc(exp_ready, 1)

        @block.gpsimd
        def _(pool):
            columns = ident[:, :].rearrange("p (q j c g) -> p q j c g", q=4, j=4, c=E // 4)
            for j in range(4):
                for c in range(E // 4):
                    g = nc.gpsimd.tensor_copy(regroup[:, :, j, :, c], columns[:, :, j, c, :].rearrange("p q g -> p g q"))
            g.then_inc(regroup_ready, 1)

        @block.tensor
        def _(pe):
            pe.wait_ge(aff_ready, 1)
            for r in range(R):
                m = nc.tensor.transpose(bk_aff[:, S * r:S * (r + 1)], aff[:, r, :, :, :].rearrange("p a b c -> p (a b c)"),
                                        ident[:, :])
            m.then_inc(aff_written, 1)
            pe.wait_ge(regroup_ready, 1)
            regrouped(pe, 1, 0, 1)

        @block.vector
        def _(dve):
            def over_experts(a):
                return a.rearrange("p (a b) -> p a b", b=1).to_broadcast([S, B, E])

            done(dve, nc.vector.tensor_reduce(top, logits[:, :, :], AX, ALU.max))
            nc.vector.tensor_tensor(shifted, logits[:, :, :], over_experts(top), ALU.subtract).then_inc(shifted_ready, 1)
            dve.wait_ge(exp_ready, 1)
            done(dve, nc.vector.tensor_reduce(total, weights, AX, ALU.add))
            done(dve, nc.vector.reciprocal(share, total))
            for r in range(R):
                at = slice(16 * r, 16 * (r + 1))
                a = nc.vector.tensor_tensor(
                    aff[:, r, :, :, :].rearrange("p q j e -> p j q e"),
                    weights[:, at, :].rearrange("p (j q) e -> p j q e", j=4),
                    share[:, at].rearrange("p (j q c) -> p j q c", j=4, c=1).to_broadcast([S, 4, 4, E]), ALU.mult)
            a.then_inc(aff_ready, 1)
            dve.wait_ge(aff_written, 1)
            done(dve, nc.vector.tensor_copy(flat(affT), bk_aff))
            for k in range(CAP // 8):
                take(dve, k, 0, 1)
            tokens(dve, 1, 0, 1)
    return take, regrouped, tokens


def experts(nc, v):
    S, B, D, E, I, CAP = (v[n] for n in ("S", "B", "D", "E", "I", "CAP"))
    x_sb, xg_hi, xg_lo, ffn_hi, ffn_lo, ident_h, iota, pick, gain, out, sem = (v[n] for n in (
        "x_sb", "xg_hi", "xg_lo", "ffn_hi", "ffn_lo", "ident_h", "iota", "pick", "gain", "out", "sem"))
    R = B // 16
    M = 4
    T = M * 4 * CAP
    IC = I // 128
    UP, DOWN = E * I, 2 * E * I

    with ExitStack() as ctx:
        def sb(name, shape, dt):
            return ctx.enter_context(nc.sbuf_tensor(name, shape, dt))

        def two(name, shape, dt):
            return [sb(f"{name}{i}", shape, dt) for i in range(2)]

        def bank(name, dt=F32):
            return ctx.enter_context(nc.psum_tensor(name, [128, 2048 // mybir.dt.size(dt)], dt))

        x_in = sb("x_in", [D, 2, 2, E, T], F16)
        hid = [[sb(f"hid{i}{j}", [128, IC, T], F16) for j in range(2)] for i in range(2)]
        silu = two("silu", [128, T], F32)
        hid_f = two("hid_f", [128, T], F32)
        y_f = sb("y_f", [128, T], F32)
        y = sb("y", [128, 2, M, D], F16)
        y_flat = sb("y_all", [128, E * 2 * M * D], F16)
        y_all = y_flat[:, :].rearrange("p (g q i m d) -> p g q i m d", g=E // 4, q=4, i=2, m=M)
        hot_t = sb("hot_t", [128, 4 * (E // 4), S], F16)
        hot = sb("hot", [S, 4 * (E // 4), 128], F16)
        hot_ahead = (hot, y_flat[:, -E * 128:].rearrange("p (a b) -> p a b", a=E))
        back = sb("back", [128, M, 4 * (E // 4), S], F16)
        bk_g, bk_u = [bank("bk_g0"), bank("bk_g1")], [bank("bk_u0"), bank("bk_u1")]
        bk_y, bk_c, bk_x = bank("bk_y2"), bank("bk_c"), bank("bk_x2")
        bk_h = bank("bk_h", F16)
        bk_q = (bk_c[:, :], bk_c[:, :], bk_y[:, :], bk_h[:, :].bitcast(F32))
        bk_ahead = (bk_x, bk_c, bk_y)
        bk_tail = (bk_c[:, :], bk_x[:, :], bk_g[0][:, :], bk_g[1][:, :])
        gate_written, up_written, down_written = sem("gate_written"), sem("up_written"), sem("down_written")
        silu_ready, hid_f_ready = sem("silu_ready"), sem("hid_f_ready")
        hid_hi_ready, hid_lo_ready = sem("hid_hi_ready"), sem("hid_lo_ready")
        y_f_ready, y_hi_ready, y_lo_ready = sem("y_f_ready"), sem("y_hi_ready"), sem("y_lo_ready")
        hot_t_ready, hot_written, hot_ready = sem("hot_t_ready"), sem("hot_written"), sem("hot_ready")
        gather_written, x_in_ready = sem("gather_written"), sem("x_in_ready")
        back_ready, scatter_written, out_ready = sem("back_ready"), sem("scatter_written"), sem("out_ready")
        y_moved, stored = sem("y_moved"), sem("stored")
        pick_ready = sem("pick_ready")

        def some(count):
            return not isinstance(count, int) or count > 0

        def rounds(eng, step):
            def one(r, gather, scatter):
                step(r, 0, 0, gather, False)
                step(r, 1, 1, gather, scatter)
                with eng.Fori(2, E - 1, 2) as e:
                    step(r, e, 0, gather, False)
                    step(r, e + 1, 1, gather, False)

            one(0, R > 1, False)
            if R > 2:
                with eng.Fori(1, R - 1, 1) as r:
                    one(r, True, True)
            if R > 1:
                one(R - 1, False, True)

        def quad_of(e, odd):
            if isinstance(e, int):
                return e // 2
            return (e - odd) // 2

        take, regrouped, tokens = routing(nc, v, y_flat[:, :].bitcast(F32), bk_u[0][:, :], bk_u[1][:, :])
        block = ctx.enter_context(nc.Block())

        @block.sync
        def _(sp):
            def move(r, e):
                sp.wait_ge(y_lo_ready, E * r + e + 1)
                sp.nop(nofuse=True)
                if e == 0:
                    if some(M * r):
                        sp.wait_ge(scatter_written, M * r)
                to = slice(CAP * (e % 4), CAP * (e % 4 + 1))
                for q in range(4):
                    sp.dma_start(y_all[to, e // 4, q, :, :, :], y[CAP * q:CAP * (q + 1), :, :, :]).then_inc(y_moved, 16)

            def store(r, m):
                sp.wait_ge(out_ready, M * r + m + 1)
                sp.nop(nofuse=True)
                b = 16 * r + 4 * m
                at = bass.ds(b, 4) if not isinstance(b, int) else slice(b, b + 4)
                sp.dma_start(out[:, at, :], x_sb[:, at, :]).then_inc(stored, 16)

            def one(r, stores):
                for e in range(E):
                    if stores and e < M:
                        store(r - 1, e)
                    move(r, e)

            one(0, False)
            with sp.Fori(1, R, 1) as r:
                one(r, True)
            for m in range(M):
                store(R - 1, m)
            sp.wait_ge(stored, 16 * R * M)

        @block.tensor
        def _(pe):
            def turn(r1, m):
                a = 4 * r1 + m
                pe.wait_ge(hot_t_ready, a + 1)
                if some(a):
                    pe.wait_ge(hot_ready, a)
                for i in range(E):
                    t = nc.tensor.transpose(bk_h[:, i * 128:(i + 1) * 128], hot_t[:, i, :], ident_h[:, :])
                t.then_inc(hot_written, 1)

            def gather(r1, m, q, ahead=False):
                a = 4 * (4 * r1 + m) + q
                pe.wait_ge(hot_ready, 4 * r1 + m + 1)
                before = a - 2 if ahead else a
                if some(before):
                    pe.wait_ge(x_in_ready, before)
                bk = bk_ahead[a % 3] if ahead else bk_x
                G = E // 4
                rhs = (hot_ahead[m % 2] if ahead else hot)[:, G * q:G * (q + 1), :].rearrange("p a b -> p (a b)")
                b = 16 * r1 + 4 * m + q
                nc.tensor.matmul(bk[:, 0:E * CAP], xg_hi[:, b, :], rhs, start=True, stop=True)
                nc.tensor.matmul(bk[:, E * CAP:2 * E * CAP], xg_lo[:, b, :], rhs,
                                 start=True, stop=True).then_inc(gather_written, 1)


            def projections(r, e, n, ic):
                k = IC * n + ic
                if ic == 0:
                    pe.wait_ge(x_in_ready, 16 * (r + 1))
                par = r % 2
                for bk, written, free, base in ((bk_g, gate_written, silu_ready, 0), (bk_u, up_written, hid_f_ready, UP)):
                    if some(k - 1):
                        pe.wait_ge(free, k - 1)
                    if isinstance(k, int) and k == 1 and base == UP:
                        pe.wait_ge(pick_ready, 1)
                    at = bass.ds(base + e * I + ic * 128, 128)
                    o = bk[ic % 2][:, :]
                    hi, lo = x_in[:, par, 0, e, :], x_in[:, par, 1, e, :]
                    nc.tensor.matmul(o, ffn_hi[:, at], hi, start=True, stop=False)
                    nc.tensor.matmul(o, ffn_lo[:, at], hi, start=False, stop=False)
                    nc.tensor.matmul(o, ffn_hi[:, at], lo, start=False, stop=True).then_inc(written, 1)

            def down(n, e, par):
                pe.wait_ge(hid_lo_ready, IC * (n + 1))
                if some(n):
                    pe.wait_ge(y_f_ready, n)
                for m in range(M):
                    for ic in range(IC):
                        at = bass.ds(DOWN + e * I + ic * D, D)
                        o = bk_y[:, m * D:(m + 1) * D]
                        hh, hl = (hid[i][par][:, ic, m * 128:(m + 1) * 128] for i in range(2))
                        nc.tensor.matmul(o, hh, ffn_hi[:, at], start=ic == 0, stop=False)
                        nc.tensor.matmul(o, hl, ffn_hi[:, at], start=False, stop=False)
                        t = nc.tensor.matmul(o, hh, ffn_lo[:, at], start=False, stop=ic == IC - 1)
                t.then_inc(down_written, 1)

            def scatter(r, m, bk, groups=range(E // 4)):
                G = E // 4
                whole = len(groups) == G
                if m == 0:
                    pe.wait_ge(y_moved, 64 * (E * r + 4 * (groups[-1] + 1)))
                a = M * r + m
                pe.wait_ge(back_ready, a + 1)
                if whole and m < 2 and some(a):
                    pe.wait_ge(out_ready, a)
                for q in range(4):
                    first, last = whole or q == 0, whole or q == 3
                    for g in groups:
                        for i in range(2):
                            t = nc.tensor.matmul(bk[:, q * D:(q + 1) * D], back[:, m, G * q + g, :],
                                                 y_all[:, g, q, i, m, :], start=first and g + i == 0,
                                                 stop=last and g == G - 1 and i == 1)
                if groups[-1] == G - 1:
                    t.then_inc(scatter_written, 1)

            def scattered(r):
                if some(M * r):
                    pe.wait_ge(out_ready, M * r)

            def step(r, e, odd, with_gather, with_scatter):
                n = E * r + e
                m = quad_of(e, odd)
                later = not isinstance(e, int) or e > 1
                projections(r, e, n, 0)
                if with_gather and odd:
                    gather(r + 1, m, 1)
                projections(r, e, n, 1)
                if with_gather:
                    if later and not odd:
                        scattered(r)
                    gather(r + 1, m, 2) if odd else turn(r + 1, m)
                projections(r, e, n, 2)
                if not (isinstance(n, int) and n == 0):
                    if later and not odd:
                        scattered(r)
                    down(n - 1, e - 1 if not isinstance(e, int) or e > 0 else E - 1, 1 - odd)
                if with_scatter:
                    scatter(r - 1, 0, bk_q[0])
                if with_gather:
                    gather(r + 1, m, 3 if odd else 0)
                projections(r, e, n, 3)
                if with_scatter:
                    scatter(r - 1, 1, bk_q[1])
                    pe.wait_ge(y_f_ready, n)
                    scatter(r - 1, 2, bk_q[2])
                    pe.wait_ge(hot_ready, min(4 * (r + 1), 4 * R) if isinstance(r, int) else 4 * r + 5)
                    scatter(r - 1, 3, bk_q[3])

            turn(0, 0)
            for m in range(M):
                for q in range(4):
                    gather(0, m, q, True)
                    if q == 1 and m < M - 1:
                        turn(0, m + 1)
            regrouped(pe, 2, 1, R)
            rounds(pe, step)
            pe.wait_ge(silu_ready, IC * E * R)
            pe.wait_ge(out_ready, M * (R - 1))
            for m in range(M):
                scatter(R - 1, m, bk_tail[m], range(0, E // 4 - 1))
            down(E * R - 1, E - 1, 1)
            for m in range(M):
                scatter(R - 1, m, bk_tail[m], range(E // 4 - 1, E // 4))

        @block.scalar
        def _(act):
            def x_in_part(r1, m, q, ahead=False):
                a = 4 * (4 * r1 + m) + q
                act.wait_ge(gather_written, a + 1)
                if some(IC * E * (r1 - 1)):
                    act.wait_ge(up_written, IC * E * (r1 - 1))
                bk = bk_ahead[a % 3] if ahead else bk_x
                for i in range(2):
                    c = nc.scalar.copy(x_in[:, r1 % 2, i, :, bass.ds(m * 128 + q * CAP, CAP)],
                                       bk[:, i * E * CAP:(i + 1) * E * CAP].rearrange("p (a b) -> p a b", a=E))
                c.then_inc(x_in_ready, 1)


            def gate(n, ic):
                k = IC * n + ic
                act.wait_ge(gate_written, k + 1)
                if some(k - 1):
                    act.wait_ge(hid_f_ready, k - 1)
                nc.scalar.activation(silu[ic % 2][:, :], bk_g[ic % 2][:, :], ACT.Silu,
                                     scale=1.0 / WSCALE).then_inc(silu_ready, 1)

            def hid_hi(n, ic, par):
                k = IC * n + ic
                act.wait_ge(hid_f_ready, k + 1)
                nc.scalar.copy(hid[0][par][:, ic, :], hid_f[ic % 2][:, :]).then_inc(hid_hi_ready, 1)

            def y_hi(n):
                act.wait_ge(y_f_ready, n + 1)
                if some(n):
                    act.wait_ge(y_moved, 64 * n)
                nc.scalar.copy(y[:, 0, :, :].rearrange("p a b -> p (a b)"), y_f[:, :]).then_inc(y_hi_ready, 1)

            def step(r, e, odd, with_gather, with_scatter):
                n = E * r + e
                m = quad_of(e, odd)
                first = isinstance(n, int) and n == 0
                if not first:
                    hid_hi(n - 1, IC - 1, 1 - odd)
                gate(n, 0)
                if with_gather and odd:
                    x_in_part(r + 1, m, 1)
                gate(n, 1)
                hid_hi(n, 0, odd)
                if with_gather and odd:
                    x_in_part(r + 1, m, 2)
                gate(n, 2)
                hid_hi(n, 1, odd)
                hid_hi(n, 2, odd)
                if with_gather and odd:
                    x_in_part(r + 1, m, 3)
                gate(n, 3)
                if not first:
                    y_hi(n - 1)
                if with_gather and not odd:
                    x_in_part(r + 1, m, 0)

            nc.scalar.activation(silu[0][:, 0:1], gain[:, 0, 0:1], ACT.Silu)
            for m in range(M):
                for q in range(4):
                    x_in_part(0, m, q, True)
            rounds(act, step)
            hid_hi(E * R - 1, IC - 1, 1)
            y_hi(E * R - 1)

        @block.gpsimd
        def _(pool):
            def hid_lo(n, ic, par):
                k = IC * n + ic
                pool.wait_ge(hid_hi_ready, k + 1)
                nc.gpsimd.tensor_tensor(hid[1][par][:, ic, :], hid_f[ic % 2][:, :], hid[0][par][:, ic, :],
                                        ALU.subtract).then_inc(hid_lo_ready, 1)

            def y_lo(n):
                pool.wait_ge(y_hi_ready, n + 1)
                part = [y[:, i, :, :].rearrange("p a b -> p (a b)") for i in range(2)]
                nc.gpsimd.tensor_tensor(part[1], y_f[:, :], part[0], ALU.subtract).then_inc(y_lo_ready, 1)

            def step(r, e, odd, with_gather, with_scatter):
                n = E * r + e
                first = isinstance(n, int) and n == 0
                if not first:
                    hid_lo(n - 1, IC - 1, 1 - odd)
                for ic in range(IC - 1):
                    hid_lo(n, ic, odd)
                if not first:
                    y_lo(n - 1)

            rounds(pool, step)
            hid_lo(E * R - 1, IC - 1, 1)
            y_lo(E * R - 1)

        @block.vector
        def _(dve):
            iota_e = iota[:, :].rearrange("p (a b) -> p a b", a=1).to_broadcast([128, E, S])

            def one_hot(dst, quad):
                return nc.vector.tensor_tensor(
                    dst, iota_e,
                    pick[:, quad, :, :].rearrange("p a (b c) -> p (a b) c", c=1).to_broadcast([128, E, S]), ALU.is_equal)

            def hot_rows(r1, m):
                a = 4 * r1 + m
                if some(a):
                    dve.wait_ge(hot_written, a)
                one_hot(hot_t[:, :, :], a).then_inc(hot_t_ready, 1)

            def hot_columns(r1, m, ahead=False):
                a = 4 * r1 + m
                dve.wait_ge(hot_written, a + 1)
                before = a - 1 if ahead else a
                if some(before):
                    dve.wait_ge(gather_written, 4 * before)
                nc.vector.tensor_copy((hot_ahead[m % 2] if ahead else hot)[:, :, :].rearrange("p a b -> p (a b)"),
                                      bk_h[:, :]).then_inc(hot_ready, 1)


            def hidden(n, ic):
                k = IC * n + ic
                dve.wait_ge(silu_ready, k + 1)
                dve.wait_ge(up_written, k + 1)
                if some(k - 1):
                    dve.wait_ge(hid_lo_ready, k - 1)
                nc.vector.tensor_tensor(hid_f[ic % 2][:, :], bk_u[ic % 2][:, :], silu[ic % 2][:, :],
                                        ALU.mult).then_inc(hid_f_ready, 1)

            def gated(n, r, e):
                dve.wait_ge(down_written, n + 1)
                if some(n):
                    dve.wait_ge(y_lo_ready, n)
                nc.vector.tensor_tensor(
                    y_f[:, :].rearrange("p (a b) -> p a b", a=M), bk_y[:, :].rearrange("p (a b) -> p a b", a=M),
                    gain[:, bass.ds(M * r, M), e].rearrange("p (a b) -> p a b", b=1).to_broadcast([128, M, D]),
                    ALU.mult).then_inc(y_f_ready, 1)

            def scatter_rows(a):
                m = a % M
                one_hot(back[:, m, :, :], a).then_inc(back_ready, 1)

            def add(r, m, bk):
                a = M * r + m
                dve.wait_ge(scatter_written, a + 1)
                at = x_sb[:, bass.ds(16 * r + 4 * m, 4), :]
                nc.vector.scalar_tensor_tensor(
                    out=at, in0=bk.rearrange("p (a b) -> p a b", a=4), scalar=1.0 / WSCALE,
                    in1=at, op0=ALU.mult, op1=ALU.add).then_inc(out_ready, 1)

            def step(r, e, odd, with_gather, with_scatter):
                n = E * r + e
                m = quad_of(e, odd)
                if with_gather and not odd:
                    hot_rows(r + 1, m)
                hidden(n, 0)
                hidden(n, 1)
                if with_gather and not odd:
                    hot_columns(r + 1, m)
                hidden(n, 2)
                if not odd and not (isinstance(n, int) and n == 0):
                    scatter_rows(M * r + m - 1)
                if not (isinstance(n, int) and n == 0):
                    if isinstance(e, int) and e == 0:
                        gated(n - 1, r - 1, E - 1)
                    else:
                        gated(n - 1, r, e - 1)
                if with_scatter:
                    add(r - 1, 0, bk_q[0])
                hidden(n, 3)
                if with_scatter:
                    for m in range(1, M):
                        add(r - 1, m, bk_q[m])

            hot_rows(0, 0)
            for m in range(M):
                hot_columns(0, m, True)
                if m < M - 1:
                    hot_rows(0, m + 1)
                take(dve, m, 1, R)
            tokens(dve, 2, 1, R)
            nc.vector.nop().then_inc(pick_ready, 1)
            rounds(dve, step)
            scatter_rows(M * R - 1)
            gated(E * R - 1, R - 1, E - 1)
            for m in range(M):
                add(R - 1, m, bk_tail[m])


def kernel(x, ctx_1024, fside_1x1xSxS2_0, L0_xattn_Wq, L0_xattn_Wk, L0_xattn_Wv, L0_xattn_Wp,
           L0_ffn_gate_w, L0_ffn_w_gate, L0_ffn_w_up, L0_ffn_w_down):
    import numpy as np
    import concourse.bacc as bacc
    from concourse.bass_utils import run_bass_kernel_spmd

    x, context, bias = (np.asarray(a) for a in (x, ctx_1024, fside_1x1xSxS2_0))
    wq, wk, wv, wp = (np.asarray(a) for a in (L0_xattn_Wq, L0_xattn_Wk, L0_xattn_Wv, L0_xattn_Wp))
    gate_w, w_gate, w_up, w_down = (np.asarray(a) for a in (
        L0_ffn_gate_w, L0_ffn_w_gate, L0_ffn_w_up, L0_ffn_w_down))
    d, e, i = x.shape[2], w_gate.shape[0], w_gate.shape[1]
    arrays = {
        "x": x.transpose(1, 0, 2),
        "ctx_t": context.transpose(2, 0, 1),
        "bias": bias[0, 0],
        "wqkv_t": np.concatenate([wq.T, wk.T, wv.T], axis=1),
        "wp_t": wp.T.reshape(-1, 128, d).transpose(1, 0, 2),
        "gate_t": gate_w.T,
        "ffn_w": np.concatenate([
            w_gate.transpose(2, 0, 1).reshape(d, e * i),
            w_up.transpose(2, 0, 1).reshape(d, e * i),
            w_down.transpose(2, 0, 1).reshape(i // 128, 128, e, d).transpose(1, 2, 0, 3).reshape(128, e * i),
        ], axis=1),
    }
    arrays = {name: np.ascontiguousarray(a) for name, a in arrays.items()}
    nc = bacc.Bacc("TRN2", target_bir_lowering=False, num_devices=1)
    args = [nc.dram_tensor(name, a.shape, mybir.dt.from_np(a.dtype), kind="ExternalInput").ap()
            for name, a in arrays.items()]
    out = nc.dram_tensor("out", arrays["x"].shape, F32, kind="ExternalOutput").ap()
    cross_attention_moe_kernel(nc, *args, out)
    got = run_bass_kernel_spmd(nc, [arrays], core_ids=[0])
    return np.ascontiguousarray(got.results[0]["out"].transpose(1, 0, 2))
```
